# Optimizing a Trainium2 kernel written in Bass

```python
import numpy as np
import jax
import jax.numpy as jnp

def _softmax(x, axis=-1):
    return jax.nn.softmax(x, axis=axis)

def _gelu(x):
    return jax.nn.gelu(x, approximate=True)

def _silu(x):
    return jax.nn.silu(x)

def _sigmoid(x):
    return jax.nn.sigmoid(x)

def _layernorm(x, axis=-1, eps=1e-05):
    m = jnp.mean(x, axis=axis, keepdims=True)
    v = jnp.var(x, axis=axis, keepdims=True)
    return (x - m) / jnp.sqrt(v + eps)

def _scatter_add(tgt, idx, src, axis=0):
    return tgt.at[idx].add(src)

def _segment_sum(src, seg, n):
    return jax.ops.segment_sum(src, seg, n)
kernel_name = 'mk_vit_tower_d1_tok_img1024_r4_7af507'

def setup_inputs(seed: int=0):
    np.random.seed(seed)
    _w = jnp.asarray

    def _rec_inputs():
        import jax
        import jax.numpy as jnp
        _rk = jax.random.key(seed)
        x = -0.00016672 + 0.999947 * jax.random.normal(jax.random.fold_in(_rk, 1), (32, 3, 96, 96), jnp.float32)
        return x
    x = _rec_inputs()

    def _L0_tok_setup():
        import jax, jax.numpy as jnp
        import numpy as np
        PATCH = 16
        key = jax.random.key(seed)
        k1, k2, k3 = jax.random.split(key, 3)
        B, C, H, Wd = (64, 3, 96, 96)
        patch_dim = C * PATCH * PATCH
        embed_dim = 256
        x = jax.random.normal(k1, (B, C, H, Wd), dtype=jnp.float32)
        W = jax.random.normal(k2, (embed_dim, patch_dim), dtype=jnp.float32) * patch_dim ** (-0.5)
        b = jax.random.normal(k3, (embed_dim,), dtype=jnp.float32) * 0.01
        return {'x': x, 'W': W, 'b': b}
    _L0_tok_all = _L0_tok_setup()
    _L0_tok_in = {k: v for k, v in _L0_tok_all.items() if k in ('W', 'b')}
    del _L0_tok_all

    def _L0_attn_setup():
        import jax, jax.numpy as jnp
        import numpy as np
        import math
        HIDDEN = 256
        HEADS = 16
        HEAD_DIM = HIDDEN // HEADS
        B, S = (2, 512)

        def _xavier(key, shape):
            fan_in, fan_out = (shape[1], shape[0])
            limit = math.sqrt(6.0 / (fan_in + fan_out))
            return jax.random.uniform(key, shape, jnp.float32, -limit, limit)
        key = jax.random.key(seed)
        ks = jax.random.split(key, 5)
        x = jax.random.normal(ks[0], (B, S, HIDDEN), jnp.float32)
        Wq = _xavier(ks[1], (HIDDEN, HIDDEN))
        Wk = _xavier(ks[2], (HIDDEN, HIDDEN))
        Wv = _xavier(ks[3], (HIDDEN, HIDDEN))
        Wo = _xavier(ks[4], (HIDDEN, HIDDEN))
        bq = jnp.zeros((HIDDEN,), jnp.float32)
        bk = jnp.zeros((HIDDEN,), jnp.float32)
        bv = jnp.zeros((HIDDEN,), jnp.float32)
        bo = jnp.zeros((HIDDEN,), jnp.float32)
        return {'x': x, 'Wq': Wq, 'bq': bq, 'Wk': Wk, 'bk': bk, 'Wv': Wv, 'bv': bv, 'Wo': Wo, 'bo': bo}
    _L0_attn_all = _L0_attn_setup()
    _L0_attn_in = {k: v for k, v in _L0_attn_all.items() if k in ('Wq', 'bq', 'Wk', 'bk', 'Wv', 'bv', 'Wo', 'bo')}
    del _L0_attn_all

    def _L0_ffn_setup():
        import jax, jax.numpy as jnp
        import numpy as np
        DIM = 256

        def _reference_tuple_inner(x, W_r, W_k, W_v, mu_r, mu_k):
            B, T, C = x.shape
            x_prev = jnp.concatenate([jnp.zeros((B, 1, C), x.dtype), x[:, :-1, :]], axis=1)
            xr = mu_r * x + (1.0 - mu_r) * x_prev
            xk = mu_k * x + (1.0 - mu_k) * x_prev
            r = jax.nn.sigmoid(jnp.einsum('btc,dc->btd', xr, W_r))
            k = jnp.einsum('btc,dc->btd', xk, W_k)
            k_act = jnp.square(jax.nn.relu(k))
            out = r * jnp.einsum('btc,dc->btd', k_act, W_v)
            new_state = x[:, -1, :]
            return (out, new_state)
        key = jax.random.key(seed)
        ks = jax.random.split(key, 6)
        B, T, C = (8, 512, DIM)
        x = jax.random.normal(ks[0], (B, T, C), dtype=jnp.float32)
        s = 1.0 / np.sqrt(C)
        W_r = jax.random.uniform(ks[1], (C, C), jnp.float32, -s, s)
        W_k = jax.random.uniform(ks[2], (C, C), jnp.float32, -s, s)
        W_v = jax.random.uniform(ks[3], (C, C), jnp.float32, -s, s)
        mu_r = jax.random.uniform(ks[4], (C,), jnp.float32)
        mu_k = jax.random.uniform(ks[5], (C,), jnp.float32)
        return {'x': x, 'W_r': W_r, 'W_k': W_k, 'W_v': W_v, 'mu_r': mu_r, 'mu_k': mu_k}
    _L0_ffn_all = _L0_ffn_setup()
    _L0_ffn_in = {k: v for k, v in _L0_ffn_all.items() if k in ('W_r', 'W_k', 'W_v', 'mu_r', 'mu_k')}
    del _L0_ffn_all
    return {'x': x, 'L0_tok_W': _L0_tok_in['W'], 'L0_tok_b': _L0_tok_in['b'], 'L0_attn_Wq': _L0_attn_in['Wq'], 'L0_attn_bq': _L0_attn_in['bq'], 'L0_attn_Wk': _L0_attn_in['Wk'], 'L0_attn_bk': _L0_attn_in['bk'], 'L0_attn_Wv': _L0_attn_in['Wv'], 'L0_attn_bv': _L0_attn_in['bv'], 'L0_attn_Wo': _L0_attn_in['Wo'], 'L0_attn_bo': _L0_attn_in['bo'], 'L0_ffn_W_r': _L0_ffn_in['W_r'], 'L0_ffn_W_k': _L0_ffn_in['W_k'], 'L0_ffn_W_v': _L0_ffn_in['W_v'], 'L0_ffn_mu_r': _L0_ffn_in['mu_r'], 'L0_ffn_mu_k': _L0_ffn_in['mu_k']}

def reference(x, L0_tok_W, L0_tok_b, L0_attn_Wq, L0_attn_bq, L0_attn_Wk, L0_attn_bk, L0_attn_Wv, L0_attn_bv, L0_attn_Wo, L0_attn_bo, L0_ffn_W_r, L0_ffn_W_k, L0_ffn_W_v, L0_ffn_mu_r, L0_ffn_mu_k):
    import jax
    import jax.numpy as jnp

    def _L0_tok_ref(x, W, b):
        import jax, jax.numpy as jnp
        import numpy as np
        PATCH = 16
        B, C, H, Wd = x.shape
        ph = pw = PATCH
        gh, gw = (H // ph, Wd // pw)
        patches = x.reshape(B, C, gh, ph, gw, pw)
        patches = patches.transpose(0, 2, 4, 1, 3, 5).reshape(B, gh * gw, C * ph * pw)
        out = jnp.einsum('bnp,dp->bnd', patches, W) + b
        return out

    def _L0_attn_ref(x, Wq, bq, Wk, bk, Wv, bv, Wo, bo):
        import jax, jax.numpy as jnp
        import numpy as np
        import math
        HIDDEN = 256
        HEADS = 16
        HEAD_DIM = HIDDEN // HEADS
        B, S = (2, 512)

        def _xavier(key, shape):
            fan_in, fan_out = (shape[1], shape[0])
            limit = math.sqrt(6.0 / (fan_in + fan_out))
            return jax.random.uniform(key, shape, jnp.float32, -limit, limit)
        b, s, d = x.shape
        h, hd = (HEADS, HEAD_DIM)
        q = (x @ Wq.T + bq).reshape(b, s, h, hd).transpose(0, 2, 1, 3)
        k = (x @ Wk.T + bk).reshape(b, s, h, hd).transpose(0, 2, 1, 3)
        v = (x @ Wv.T + bv).reshape(b, s, h, hd).transpose(0, 2, 1, 3)
        scores = jnp.einsum('bhqd,bhkd->bhqk', q, k) / math.sqrt(hd)
        causal = jnp.tril(jnp.ones((s, s), bool))
        scores = jnp.where(causal, scores, -jnp.inf)
        attn = jax.nn.softmax(scores, axis=-1)
        out = jnp.einsum('bhqk,bhkd->bhqd', attn, v)
        out = out.transpose(0, 2, 1, 3).reshape(b, s, d)
        return out @ Wo.T + bo

    def _L0_ffn_ref(x, W_r, W_k, W_v, mu_r, mu_k):
        import jax, jax.numpy as jnp
        import numpy as np
        DIM = 256

        def _reference_tuple_inner(x, W_r, W_k, W_v, mu_r, mu_k):
            B, T, C = x.shape
            x_prev = jnp.concatenate([jnp.zeros((B, 1, C), x.dtype), x[:, :-1, :]], axis=1)
            xr = mu_r * x + (1.0 - mu_r) * x_prev
            xk = mu_k * x + (1.0 - mu_k) * x_prev
            r = jax.nn.sigmoid(jnp.einsum('btc,dc->btd', xr, W_r))
            k = jnp.einsum('btc,dc->btd', xk, W_k)
            k_act = jnp.square(jax.nn.relu(k))
            out = r * jnp.einsum('btc,dc->btd', k_act, W_v)
            new_state = x[:, -1, :]
            return (out, new_state)
        return _reference_tuple_inner(x, W_r, W_k, W_v, mu_r, mu_k)[0]
    h = _L0_tok_ref(x, L0_tok_W, L0_tok_b)
    h = h + _L0_attn_ref(_layernorm(h, axis=-1), L0_attn_Wq, L0_attn_bq, L0_attn_Wk, L0_attn_bk, L0_attn_Wv, L0_attn_bv, L0_attn_Wo, L0_attn_bo)
    h = h + _L0_ffn_ref(_layernorm(h, axis=-1), L0_ffn_W_r, L0_ffn_W_k, L0_ffn_W_v, L0_ffn_mu_r, L0_ffn_mu_k)
    return h

_drawn_inputs = setup_inputs


def setup_inputs(seed=0):
    import zlib

    import numpy as np

    out = dict(_drawn_inputs(seed))
    spreads = {'L0_attn_bq': (0.0, 0.3),
     'L0_attn_bk': (0.0, 0.8),
     'L0_attn_bv': (0.0, 0.1),
     'L0_attn_bo': (0.0, 0.1)}
    factors = {'L0_tok_b': 4.177, 'L0_ffn_W_r': 3.371, 'L0_ffn_mu_r': 7.315}
    for name, (base, spread) in spreads.items():
        noise = np.random.default_rng([zlib.crc32(name.encode()), seed]).standard_normal(out[name].shape)
        drawn = base * np.exp(spread * noise) if base else spread * noise
        out[name] = jnp.asarray(drawn.astype(out[name].dtype))
    for name, factor in factors.items():
        out[name] = (out[name] * factor).astype(out[name].dtype)
    return out
```

```python
from contextlib import ExitStack

import concourse.bass as bass
from concourse import mybir

BATCH, CHANNELS, IMAGE, PATCH = 32, 3, 96, 16
GRID = IMAGE // PATCH
SEQ = GRID * GRID
TOKENS = BATCH * SEQ
PIXELS = CHANNELS * PATCH * PATCH
P = 128
DIM, HEADS = 256, 16
HEAD_DIM = DIM // HEADS
FC = DIM // P
PC = PIXELS // P
TILES = TOKENS // P
LN_EPS = 1e-5
MASKED = -1e38

GROUP = 8 * SEQ
GROUPS = TOKENS // GROUP
HALF = P // 2
PAIRS = BATCH // 2
QUAD = HALF // HEAD_DIM
HEAD_PAIRS = HEADS // 2
QUADS_V = BATCH // 4
PAD = HALF - SEQ
MIX_BATCHES = [0, 10, 21, 32]
MIX_TILES = [0, 2, 5, 9]
CONSTS = P + SEQ + QUAD

INPUTS = ["patches", "w_tok", "w_q", "w_k", "w_v", "w_o", "w_r", "w_fk", "w_fv",
          "b_tok", "b_o", "b_q", "b_k", "b_v", "mu_r", "mu_k", "consts"]


def vit_tower(nc, patches, w_tok, w_q, w_k, w_v, w_o, w_r, w_fk, w_fv,
              b_tok, b_o, b_q, b_k, b_v, mu_r, mu_k, consts, out):
    f32, bf16 = mybir.dt.float32, mybir.dt.bfloat16
    ALU, ACT, AX = mybir.AluOpType, mybir.ActivationFunctionType, mybir.AxisListType

    ctx = ExitStack()
    with ctx:
        def sb(name, shape, dt=f32):
            return ctx.enter_context(nc.sbuf_tensor(name, shape, dt))

        def sem(name):
            return ctx.enter_context(nc.semaphore(name))

        pixels = sb("pixels", [P, TILES * PC * P])
        pix = pixels[:, :].rearrange("p (t c n) -> p t c n", t=TILES, c=PC)
        mixed = pixels[:, 0:2 * FC * TOKENS].rearrange("p (w c n) -> p w c n", w=2, c=FC)
        keys_sq = pixels[:, 2 * FC * TOKENS:3 * FC * TOKENS].rearrange("p (c n) -> p c n", c=FC)
        tok_w = sb("tok_w", [P, PC, DIM])
        wq, wk, wv, wo = (sb(n, [P, FC, DIM]) for n in ("wq", "wk", "wv", "wo"))
        wr, wfk, wfv = (sb(n, [P, FC, DIM]) for n in ("wr", "wfk", "wfv"))
        tok_bias, o_bias = sb("tok_bias", [P, DIM]), sb("o_bias", [P, DIM])
        cols = sb("cols", [P, 5, FC])
        bq, bk, bv, mu = cols[:, 0, :], cols[:, 1, :], cols[:, 2, :], cols[:, 3:5, :]
        one_less_mu = sb("one_less_mu", [P, 2, FC])
        const = sb("const", [P, CONSTS])
        ident = const[:, 0:P]
        causal = const[:, P:P + SEQ]
        head_mask = const[:, P + SEQ:CONSTS]
        ident_bf = sb("ident_bf", [P, P], bf16)
        causal_bf = sb("causal_bf", [P, 8, SEQ], bf16)
        power = sb("power", [P, 1])
        h = sb("h", [P, TILES, DIM])
        stats = sb("stats", [P, 2, TILES, 6])
        moments = sb("moments", [P, 2, TILES, 2])
        var_eps = sb("var_eps", [P, 2, TILES])
        rstd = sb("rstd", [P, 2, TILES])
        normed = sb("normed", [P, 2, DIM])
        yT = sb("yT", [P, FC, TOKENS + PAD])
        qT = sb("qT", [P, FC, TOKENS])
        km = sb("km", [P, FC, QUAD, TOKENS])
        vb = sb("vb", [P, BATCH, HEAD_PAIRS, 2 * HEAD_DIM])
        diff = sb("diff", [P, 2, HEADS, SEQ])
        probs = sb("probs", [P, 3, HEADS, HALF])
        row_max = sb("row_max", [P, 2, HEADS])
        row_sum = sb("row_sum", [P, 2, HEADS])
        row_inv = sb("row_inv", [P, 2, HEADS])
        pT = sb("pT", [P, 2, HEAD_PAIRS, 2, SEQ])
        oT = sb("oT", [P, FC, TOKENS])
        gate = sb("gate", [P, 2, DIM])
        relu = sb("relu", [P, 2, 512])
        final = sb("final", [P, 2, DIM])

        bank = [ctx.enter_context(nc.psum_tensor(f"bank{i}", [P, 512], f32)) for i in range(8)]

        dma_pix = [sem(f"dma_pix{t}") for t in range(TILES)]
        dma_wtok, dma_wqk, dma_wv, dma_wlate = sem("dma_wtok"), sem("dma_wqk"), sem("dma_wv"), sem("dma_wlate")
        dma_const, dma_bias = sem("dma_const"), sem("dma_bias")
        set_up, zeroed = sem("set_up"), sem("zeroed")
        embedded, h_ready = sem("embedded"), sem("h_ready")
        bn_done, stats_ready, eps_added, rstd_ready = sem("bn_done"), sem("stats_ready"), sem("eps_added"), sem("rstd_ready")
        normed_ready, norm_transposed, yT_ready = sem("normed_ready"), sem("norm_transposed"), sem("yT_ready")
        resid_ready = sem("resid_ready")
        qk_done, q_ready, k_ready = sem("qk_done"), sem("q_ready"), sem("k_ready")
        v_done, v_even_ready, v_odd_ready = sem("v_done"), sem("v_even_ready"), sem("v_odd_ready")
        scores_done, max_ready, diff_ready = sem("scores_done"), sem("max_ready"), sem("diff_ready")
        exp_ready, sum_ready, inv_ready, probs_ready = sem("exp_ready"), sem("sum_ready"), sem("inv_ready"), sem("probs_ready")
        lo_transposed, hi_transposed = sem("lo_transposed"), sem("hi_transposed")
        pT_lo_ready, pT_hi_ready = sem("pT_lo_ready"), sem("pT_hi_ready")
        attended, oT_ready = sem("attended"), sem("oT_ready")
        projected, mu_scaled, mix_ready = sem("projected"), sem("mu_scaled"), sem("mix_ready")
        fk_done, relu_ready, sq_ready = sem("fk_done"), sem("relu_ready"), sem("sq_ready")
        r_done, gate_ready, fv_done, gated, final_ready = (sem("r_done"), sem("gate_ready"), sem("fv_done"),
                                                           sem("gated"), sem("final_ready"))
        stored = [sem("stored_even"), sem("stored_odd")]

        def pair_place(p):
            half, chunk, m = p // 4, (p // 2) % 2, p % 2
            return chunk, (half * 2 + m) * 32, chunk * 4 + half * 2 + m

        def lo_hi(p):
            return bank[4 + p // 4][:, (p % 4) * P:(p % 4 + 1) * P]

        block = ctx.enter_context(nc.Block())

        @block.sync
        def _(sp):
            sp.dma_start(tok_w[:], w_tok).then_inc(dma_wtok, 16)
            for t in range(TILES):
                sp.dma_start(pix[:, t], patches[t]).then_inc(dma_pix[t], 16)
            for dst, src in ((wo, w_o), (wr, w_r), (wfk, w_fk), (wfv, w_fv)):
                sp.dma_start(dst[:], src).then_inc(dma_wlate, 16)
            for t in range(TILES):
                sp.wait_ge(final_ready, t + 1)
                sp.dma_start(out[t * P:(t + 1) * P, :], final[:, t % 2]).then_inc(stored[t % 2], 16)
            sp.wait_ge(stored[0], 16 * (TILES - TILES // 2))
            sp.wait_ge(stored[1], 16 * (TILES // 2))

        @block.scalar
        def _(act):
            act.dma_start(const[:], consts).then_inc(dma_const, 16)
            act.dma_start(tok_bias[:], b_tok.to_broadcast([P, DIM])).then_inc(dma_bias, 16)
            act.dma_start(o_bias[:], b_o.to_broadcast([P, DIM])).then_inc(dma_bias, 16)
            for n, src in enumerate((b_q, b_k, b_v, mu_r, mu_k)):
                act.dma_start(cols[:, n], src).then_inc(dma_bias, 16)
            act.dma_start(wq[:], w_q).then_inc(dma_wqk, 16)
            act.dma_start(wk[:], w_k).then_inc(dma_wqk, 16)
            act.dma_start(wv[:], w_v).then_inc(dma_wv, 16)

            for t in range(TILES):
                act.wait_ge(norm_transposed, t + 1)
                nc.scalar.activation(yT[:, :, t * P:(t + 1) * P],
                                     bank[4 + t % 2][:, 0:DIM].rearrange("p (c n) -> p c n", c=FC),
                                     ACT.Copy).then_inc(yT_ready, 1)
            act.wait_ge(dma_bias, 7 * 16)
            for g in range(GROUPS):
                for c in range(FC):
                    act.wait_ge(qk_done, (g * FC + c) * 2 + 1)
                    nc.scalar.activation(qT[:, c, g * GROUP:(g + 1) * GROUP], bank[6][:, 0:GROUP],
                                         ACT.Identity, bias=bq[:, c:c + 1]).then_inc(q_ready, 1)
            act.wait_ge(zeroed, 2)
            for n in range(QUADS_V):
                act.wait_ge(v_done, n + 1)
                nc.scalar.activation(vb[HALF:P, 4 * n:4 * n + 4, :, HEAD_DIM:],
                                     bank[n % 2][HALF:P, :].rearrange("p (b h d) -> p b h d", b=4, d=HEAD_DIM),
                                     ACT.Copy).then_inc(v_odd_ready, 1)
            for i in range(PAIRS + 3):
                if i < PAIRS:
                    act.wait_ge(diff_ready, i + 1)
                    if i >= 3:
                        act.wait_ge(hi_transposed, i - 2)
                    nc.scalar.activation(probs[:, i % 3, :, 0:SEQ], diff[:, i % 2], ACT.Exp,
                                         scale=HEAD_DIM ** -0.5).then_inc(exp_ready, 1)
                if 2 <= i < PAIRS + 2:
                    j = i - 2
                    act.wait_ge(lo_transposed, j + 1)
                    if j >= 2:
                        act.wait_ge(attended, j - 1)
                    nc.scalar.activation(pT[:, j % 2, 0:4],
                                         bank[4][:, :].rearrange("p (h b q) -> p h b q", h=4, b=2)[:, :, :, 0:SEQ],
                                         ACT.Copy).then_inc(pT_lo_ready, 1)
                if i >= 3:
                    j = i - 3
                    act.wait_ge(attended, j + 1)
                    for c in range(FC):
                        last = nc.scalar.activation(oT[:, c, j * 2 * SEQ:(j + 1) * 2 * SEQ],
                                                    bank[6 + j % 2][:, c * 2 * SEQ:(c + 1) * 2 * SEQ],
                                                    ACT.Identity, bias=bv[:, c:c + 1])
                    last.then_inc(oT_ready, 1)
            def mix_scale(u):
                lo, hi = MIX_BATCHES[u] * SEQ, MIX_BATCHES[u + 1] * SEQ
                for w in range(2):
                    for c in range(FC):
                        last = nc.scalar.activation(mixed[:, w, c, lo:hi], yT[:, c, lo:hi], ACT.Copy,
                                                    scale=mu[:, w, c:c + 1])
                last.then_inc(mu_scaled, 1)

            def relus(u):
                n = (MIX_BATCHES[u + 1] - MIX_BATCHES[u]) * SEQ
                for c in range(FC):
                    act.wait_ge(fk_done, FC * u + c + 1)
                    if FC * u + c >= 2:
                        act.wait_ge(sq_ready, FC * u + c - 1)
                    nc.scalar.activation(relu[:, c, 0:n], bank[6 + c][:, 0:n], ACT.Relu).then_inc(relu_ready, 1)

            def gates(u):
                for t in range(MIX_TILES[u], MIX_TILES[u + 1]):
                    act.wait_ge(r_done, t + 1)
                    if t >= 2:
                        act.wait_ge(gated, t - 1)
                    nc.scalar.activation(gate[:, t % 2], bank[2 + t % 2][:, 0:DIM], ACT.Tanh,
                                         scale=0.5).then_inc(gate_ready, 1)

            for t in range(TILES):
                act.wait_ge(norm_transposed, TILES + t + 1)
                nc.scalar.activation(yT[:, :, t * P:(t + 1) * P],
                                     bank[4 + t % 2][:, 0:DIM].rearrange("p (c n) -> p c n", c=FC),
                                     ACT.Copy).then_inc(yT_ready, 1)
                if t in (2, 5, 8):
                    act.wait_ge(yT_ready, TILES + t + 1)
                    mix_scale(t // 3)
            for u in range(3):
                relus(u)
                gates(u)

        @block.gpsimd
        def _(pool):
            nc.gpsimd.memset(power[:], -0.5).then_inc(zeroed, 1)
            nc.gpsimd.memset(vb[:], 0.0).then_inc(zeroed, 1)
            pool.wait_ge(zeroed, 2)

            def rstds(which, t):
                n = which * TILES + t
                pool.wait_ge(stats_ready, n + 1)
                nc.gpsimd.tensor_scalar(var_eps[:, which, t:t + 1], moments[:, which, t, 1:2], LN_EPS, None,
                                        ALU.add).then_inc(eps_added, 1)
                pool.wait_ge(eps_added, n + 1)
                nc.gpsimd.tensor_tensor(rstd[:, which, t:t + 1], var_eps[:, which, t:t + 1], power[:],
                                        ALU.pow).then_inc(rstd_ready, 1)

            pool.wait_ge(dma_bias, 7 * 16)
            for t in range(TILES + 1):
                if t < TILES:
                    rstds(0, t)
                if t >= 1:
                    pool.wait_ge(normed_ready, t)
                    nc.gpsimd.tensor_tensor(h[:, t - 1], h[:, t - 1], o_bias[:], ALU.add).then_inc(resid_ready, 1)
            for i in range(PAIRS):
                pool.wait_ge(inv_ready, i + 1)
                nc.gpsimd.tensor_tensor(probs[:, i % 3, :, 0:SEQ], probs[:, i % 3, :, 0:SEQ],
                                        row_inv[:, i % 2].unsqueeze(2).to_broadcast([P, HEADS, SEQ]),
                                        ALU.mult).then_inc(probs_ready, 1)
            for t in range(TILES):
                rstds(1, t)
            for u in range(3):
                lo, hi = MIX_BATCHES[u] * SEQ, MIX_BATCHES[u + 1] * SEQ
                for c in range(FC):
                    pool.wait_ge(relu_ready, FC * u + c + 1)
                    nc.gpsimd.tensor_tensor(keys_sq[:, c, lo:hi], relu[:, c, 0:hi - lo], relu[:, c, 0:hi - lo],
                                            ALU.mult).then_inc(sq_ready, 1)

        @block.vector
        def _(dve):
            nc.vector.memset(probs[:], 0.0).then_inc(set_up, 1)
            nc.vector.memset(yT[:, :, TOKENS:], 0.0).then_inc(set_up, 1)
            dve.wait_ge(dma_const, 16)
            nc.vector.tensor_copy(ident_bf[:], ident).then_inc(set_up, 1)
            nc.vector.tensor_copy(causal_bf[:], causal.unsqueeze(1).to_broadcast([P, 8, SEQ])).then_inc(set_up, 1)
            dve.wait_ge(dma_bias, 7 * 16)
            nc.vector.tensor_scalar(one_less_mu[:], mu, -1.0, 1.0, ALU.mult, ALU.add).then_inc(set_up, 1)

            def statistics(which, t):
                n = which * TILES + t
                dve.wait_ge(h_ready, n + 1)
                nc.vector.bn_stats(stats[:, which, t], h[:, t]).then_inc(bn_done, 1)
                dve.wait_ge(bn_done, n + 1)
                nc.vector.bn_aggr(moments[:, which, t], stats[:, which, t]).then_inc(stats_ready, 1)

            def normalise(which, t):
                n = which * TILES + t
                dve.wait_ge(rstd_ready, n + 1)
                if n >= 2:
                    dve.wait_ge(norm_transposed, n - 1)
                nc.vector.tensor_scalar(normed[:, n % 2], h[:, t], moments[:, which, t, 0:1],
                                        rstd[:, which, t:t + 1], ALU.subtract, ALU.mult).then_inc(normed_ready, 1)

            for t in range(TILES + 1):
                if t < TILES:
                    dve.wait_ge(embedded, t + 1)
                    nc.vector.tensor_tensor(h[:, t], bank[t % 4][:, 0:DIM], tok_bias[:],
                                            ALU.add).then_inc(h_ready, 1)
                    statistics(0, t)
                if t >= 1:
                    normalise(0, t - 1)
            for g in range(GROUPS):
                for c in range(FC):
                    dve.wait_ge(qk_done, (g * FC + c) * 2 + 2)
                    for m in range(QUAD):
                        last = nc.vector.tensor_scalar(km[:, c, m, g * GROUP:(g + 1) * GROUP], bank[7][:, 0:GROUP],
                                                       bk[:, c:c + 1], head_mask[:, m:m + 1], ALU.add, ALU.mult)
                    last.then_inc(k_ready, 1)
            dve.wait_ge(zeroed, 2)
            for n in range(QUADS_V):
                dve.wait_ge(v_done, n + 1)
                nc.vector.tensor_copy(vb[0:HALF, 4 * n:4 * n + 4, :, 0:HEAD_DIM],
                                      bank[n % 2][0:HALF, :].rearrange("p (b h d) -> p b h d", b=4, d=HEAD_DIM)
                                      ).then_inc(v_even_ready, 1)

            def scores(i, half):
                return bank[2 * (i % 2) + half][:, 0:8 * SEQ].rearrange("p (s k) -> p s k", k=SEQ)

            for i in range(PAIRS + 2):
                if i < PAIRS:
                    dve.wait_ge(scores_done, i + 1)
                    if i >= 2:
                        dve.wait_ge(diff_ready, i - 1)
                    for half in range(2):
                        last = nc.vector.tensor_reduce(row_max[:, i % 2, 8 * half:8 * half + 8], scores(i, half),
                                                       AX.X, ALU.max)
                    last.then_inc(max_ready, 1)
                    dve.wait_ge(max_ready, i + 1)
                    if i >= 2:
                        dve.wait_ge(exp_ready, i - 1)
                    for half in range(2):
                        last = nc.vector.tensor_tensor(
                            diff[:, i % 2, 8 * half:8 * half + 8], scores(i, half),
                            row_max[:, i % 2, 8 * half:8 * half + 8].unsqueeze(2).to_broadcast([P, 8, SEQ]),
                            ALU.subtract)
                    last.then_inc(diff_ready, 1)
                if 1 <= i < PAIRS + 1:
                    j = i - 1
                    dve.wait_ge(exp_ready, j + 1)
                    nc.vector.tensor_reduce(row_sum[:, j % 2], probs[:, j % 3, :, 0:SEQ], AX.X,
                                            ALU.add).then_inc(sum_ready, 1)
                    dve.wait_ge(sum_ready, j + 1)
                    if j >= 2:
                        dve.wait_ge(probs_ready, j - 1)
                    nc.vector.reciprocal(row_inv[:, j % 2], row_sum[:, j % 2]).then_inc(inv_ready, 1)
                if i >= 2:
                    j = i - 2
                    dve.wait_ge(hi_transposed, j + 1)
                    if j >= 2:
                        dve.wait_ge(attended, j - 1)
                    nc.vector.tensor_copy(pT[:, j % 2, 4:8],
                                          bank[5][:, :].rearrange("p (h b q) -> p h b q", h=4, b=2)[:, :, :, 0:SEQ]
                                          ).then_inc(pT_hi_ready, 1)

            for t in range(TILES + 1):
                if t < TILES:
                    dve.wait_ge(projected, t + 1)
                    dve.wait_ge(resid_ready, t + 1)
                    nc.vector.tensor_tensor(h[:, t], bank[t % 4][:, 0:DIM], h[:, t], ALU.add).then_inc(h_ready, 1)
                    statistics(1, t)
                if t >= 1:
                    normalise(1, t - 1)
            for u in range(3):
                lo, hi = MIX_BATCHES[u] * SEQ, MIX_BATCHES[u + 1] * SEQ
                dve.wait_ge(mu_scaled, u + 1)
                dve.wait_ge(set_up, 5)
                for w in range(2):
                    for c in range(FC):
                        here = mixed[:, w, c, lo:hi].rearrange("p (b q) -> p b q", q=SEQ)[:, :, 1:SEQ]
                        before = yT[:, c, lo:hi].rearrange("p (b q) -> p b q", q=SEQ)[:, :, 0:SEQ - 1]
                        last = nc.vector.scalar_tensor_tensor(here, before, one_less_mu[:, w, c:c + 1], here,
                                                              ALU.mult, ALU.add)
                last.then_inc(mix_ready, 1)
            for t in range(TILES):
                dve.wait_ge(fv_done, t + 1)
                dve.wait_ge(gate_ready, t + 1)
                if t >= 2:
                    dve.wait_ge(stored[t % 2], 16 * (t // 2))
                nc.vector.scalar_tensor_tensor(final[:, t % 2], gate[:, t % 2], 1.0, bank[t % 2][:, 0:DIM],
                                               ALU.add, ALU.mult).then_inc(gated, 1)
                dve.wait_ge(gated, t + 1)
                nc.vector.scalar_tensor_tensor(final[:, t % 2], final[:, t % 2], 0.5, h[:, t],
                                               ALU.mult, ALU.add).then_inc(final_ready, 1)

        @block.tensor
        def _(pe):
            def transpose_norm(which, t):
                n = which * TILES + t
                pe.wait_ge(normed_ready, n + 1)
                if n >= 2:
                    pe.wait_ge(yT_ready, n - 1)
                for c in range(FC):
                    last = nc.tensor.transpose(bank[4 + t % 2][:, c * P:(c + 1) * P],
                                               normed[:, n % 2, c * P:(c + 1) * P], ident)
                last.then_inc(norm_transposed, 1)

            pe.wait_ge(dma_wtok, 16)
            pe.wait_ge(dma_const, 16)
            for t in range(TILES + 2):
                if t < TILES:
                    pe.wait_ge(dma_pix[t], 16)
                    if t >= 4:
                        pe.wait_ge(h_ready, t - 3)
                    for c in range(PC):
                        last = nc.tensor.matmul(bank[t % 4][:, 0:DIM], pix[:, t, c], tok_w[:, c],
                                                start=(c == 0), stop=(c == PC - 1))
                    last.then_inc(embedded, 1)
                if t >= 2:
                    transpose_norm(0, t - 2)
            pe.wait_ge(dma_wqk, 32)
            for g in range(GROUPS):
                pe.wait_ge(yT_ready, -(-(g + 1) * GROUP // P))
                for c in range(FC):
                    for k, w in enumerate((wq, wk)):
                        if g or c:
                            pe.wait_ge((q_ready, k_ready)[k], g * FC + c)
                        for f in range(FC):
                            last = nc.tensor.matmul(bank[6 + k][:, 0:GROUP], w[:, f, c * P:(c + 1) * P],
                                                    yT[:, f, g * GROUP:(g + 1) * GROUP],
                                                    start=(f == 0), stop=(f == FC - 1))
                        last.then_inc(qk_done, 1)
            pe.wait_ge(dma_wv, 16)
            pe.wait_ge(set_up, 5)
            pe.wait_ge(h_ready, TILES)
            for n in range(QUADS_V):
                if n >= 2:
                    pe.wait_ge(v_even_ready, n - 1)
                    pe.wait_ge(v_odd_ready, n - 1)
                for b in range(4):
                    tok = (4 * n + b) * SEQ
                    for f in range(FC):
                        for odd in range(2):
                            heads = wv[:, f].rearrange("p (h o d) -> p h o d", o=2, d=HEAD_DIM)[:, :, odd]
                            last = nc.tensor.matmul(bank[n % 2][odd * HALF:(odd + 1) * HALF, b * P:(b + 1) * P],
                                                    yT[:, f, tok:tok + HALF], heads,
                                                    start=(f == 0), stop=(f == FC - 1))
                last.then_inc(v_done, 1)

            def score(i):
                if i < 2:
                    pe.wait_ge(v_even_ready, QUADS_V)
                    pe.wait_ge(v_odd_ready, QUADS_V)
                    pe.wait_ge(q_ready, GROUPS * FC)
                    pe.wait_ge(k_ready, GROUPS * FC)
                else:
                    pe.wait_ge(diff_ready, i - 1)
                for half in range(2):
                    nc.tensor.matmul(bank[2 * (i % 2) + half][:, 0:8 * SEQ], ident_bf[:],
                                     causal_bf[:].rearrange("p s k -> p (s k)"), start=True, stop=False,
                                     skip_group_check=True)
                for c in range(FC):
                    for half in range(2):
                        for b in range(2):
                            tok = (2 * i + b) * SEQ
                            rows = slice(half * HALF, (half + 1) * HALF)
                            last = nc.tensor.matmul(
                                bank[2 * (i % 2) + half][b * HALF:b * HALF + SEQ, c * 4 * SEQ:(c + 1) * 4 * SEQ],
                                qT[rows, c, tok:tok + SEQ], km[rows, c, :, tok:tok + SEQ],
                                start=False, stop=True, skip_group_check=True)
                last.then_inc(scores_done, 1)

            def transpose_probs(i):
                pe.wait_ge(probs_ready, i + 1)
                if i >= 1:
                    pe.wait_ge(pT_lo_ready, i)
                    pe.wait_ge(pT_hi_ready, i)
                else:
                    pe.wait_ge(yT_ready, TILES)
                for p in range(HEAD_PAIRS):
                    last = nc.tensor.transpose(lo_hi(p), probs[:, i % 3, 2 * p:2 * p + 2].rearrange("p h k -> p (h k)"),
                                               ident)
                    if p == 3:
                        last.then_inc(lo_transposed, 1)
                last.then_inc(hi_transposed, 1)

            def attend(i):
                pe.wait_ge(pT_lo_ready, i + 1)
                pe.wait_ge(pT_hi_ready, i + 1)
                if i >= 2:
                    pe.wait_ge(oT_ready, i - 1)
                for b in range(2):
                    for p in range(HEAD_PAIRS):
                        c, row, true_pair = pair_place(p)
                        last = nc.tensor.matmul(
                            bank[6 + i % 2][row:row + 32, (c * 2 + b) * SEQ:(c * 2 + b + 1) * SEQ],
                            vb[:, 2 * i + b, true_pair], pT[:, i % 2, p, b], start=True, stop=True,
                            tile_position=(0, row), skip_group_check=True)
                last.then_inc(attended, 1)

            for i in range(PAIRS + 3):
                if i < PAIRS:
                    score(i)
                if i >= 3:
                    attend(i - 3)
                if 2 <= i < PAIRS + 2:
                    transpose_probs(i - 2)
            pe.wait_ge(dma_wlate, 4 * 16)
            pe.wait_ge(diff_ready, PAIRS)
            pe.wait_ge(pT_lo_ready, PAIRS)
            pe.wait_ge(pT_hi_ready, PAIRS)
            for t in range(TILES + 2):
                if t < TILES:
                    pe.wait_ge(oT_ready, -(-(t + 1) * P // (2 * SEQ)))
                    if t >= 4:
                        pe.wait_ge(h_ready, TILES + t - 3)
                    for f in range(FC):
                        last = nc.tensor.matmul(bank[t % 4][:, 0:DIM], oT[:, f, t * P:(t + 1) * P], wo[:, f],
                                                start=(f == 0), stop=(f == FC - 1))
                    last.then_inc(projected, 1)
                if t >= 2:
                    transpose_norm(1, t - 2)
            pe.wait_ge(h_ready, 2 * TILES)
            pe.wait_ge(oT_ready, PAIRS)
            for u in range(3):
                lo, hi = MIX_BATCHES[u] * SEQ, MIX_BATCHES[u + 1] * SEQ
                tiles = range(MIX_TILES[u], MIX_TILES[u + 1])
                pe.wait_ge(mix_ready, u + 1)
                for c in range(FC):
                    if u:
                        pe.wait_ge(relu_ready, FC * (u - 1) + c + 1)
                    for f in range(FC):
                        last = nc.tensor.matmul(bank[6 + c][:, 0:hi - lo], wfk[:, f, c * P:(c + 1) * P],
                                                mixed[:, 1, f, lo:hi], start=(f == 0), stop=(f == FC - 1))
                    last.then_inc(fk_done, 1)
                for t in tiles:
                    if t >= 2:
                        pe.wait_ge(gate_ready, t - 1)
                    for f in range(FC):
                        last = nc.tensor.matmul(bank[2 + t % 2][:, 0:DIM], mixed[:, 0, f, t * P:(t + 1) * P],
                                                wr[:, f], start=(f == 0), stop=(f == FC - 1))
                    last.then_inc(r_done, 1)
                pe.wait_ge(sq_ready, FC * (u + 1))
                for t in tiles:
                    if t >= 2:
                        pe.wait_ge(gated, t - 1)
                    for f in range(FC):
                        last = nc.tensor.matmul(bank[t % 2][:, 0:DIM], keys_sq[:, f, t * P:(t + 1) * P],
                                                wfv[:, f], start=(f == 0), stop=(f == FC - 1))
                    last.then_inc(fv_done, 1)


def kernel(x, L0_tok_W, L0_tok_b, L0_attn_Wq, L0_attn_bq, L0_attn_Wk, L0_attn_bk, L0_attn_Wv, L0_attn_bv,
           L0_attn_Wo, L0_attn_bo, L0_ffn_W_r, L0_ffn_W_k, L0_ffn_W_v, L0_ffn_mu_r, L0_ffn_mu_k):
    import numpy as np
    import concourse.bacc as bacc
    from concourse.bass_utils import run_bass_kernel_spmd

    def weight(w, chunks):
        return np.ascontiguousarray(np.asarray(w).T.reshape(chunks, P, DIM).transpose(1, 0, 2))

    def column(v):
        return np.ascontiguousarray(np.asarray(v).reshape(FC, P).T)

    pixels = np.asarray(x).reshape(BATCH, CHANNELS, GRID, PATCH, GRID, PATCH).transpose(1, 3, 5, 0, 2, 4)
    pixels = pixels.reshape(PC, P, TILES, P).transpose(2, 1, 0, 3)

    row = np.arange(P)[:, None]
    blocked = (np.arange(SEQ)[None, :] > row % HALF) & (row % HALF < SEQ)
    consts = np.concatenate([np.eye(P), np.where(blocked, MASKED, 0.0),
                             row // HEAD_DIM % QUAD == np.arange(QUAD)[None, :]], axis=1).astype(np.float32)

    arrays = dict(zip(INPUTS, [
        np.ascontiguousarray(pixels), weight(L0_tok_W, PC),
        *(weight(w, FC) for w in (L0_attn_Wq, L0_attn_Wk, L0_attn_Wv, L0_attn_Wo, L0_ffn_W_r, L0_ffn_W_k, L0_ffn_W_v)),
        np.asarray(L0_tok_b).reshape(1, DIM), np.asarray(L0_attn_bo).reshape(1, DIM),
        *(column(v) for v in (L0_attn_bq, L0_attn_bk, L0_attn_bv, L0_ffn_mu_r, L0_ffn_mu_k)), consts]))

    nc = bacc.Bacc("TRN2", target_bir_lowering=False, num_devices=1)
    args = [nc.dram_tensor(n, a.shape, mybir.dt.from_np(a.dtype), kind="ExternalInput").ap()
            for n, a in arrays.items()]
    out = nc.dram_tensor("out", (TOKENS, DIM), mybir.dt.float32, kind="ExternalOutput").ap()
    vit_tower(nc, *args, out)
    result = run_bass_kernel_spmd(nc, [arrays], core_ids=[0])
    return result.results[0]["out"].reshape(BATCH, SEQ, DIM)
```

```python
from contextlib import ExitStack

import concourse.bass as bass
from concourse import mybir

BATCH, CHANNELS, IMAGE, PATCH = 32, 3, 96, 16
GRID = IMAGE // PATCH
SEQ = GRID * GRID
TOKENS = BATCH * SEQ
PIXELS = CHANNELS * PATCH * PATCH
P = 128
DIM, HEADS = 256, 16
HEAD_DIM = DIM // HEADS
FC = DIM // P
PC = PIXELS // P
TILES = TOKENS // P
LN_EPS = 1e-5
MASKED = -1e38

GB = 8
GROUP = GB * SEQ
GROUPS = TOKENS // GROUP
HALF = P // 2
ROWS = HALF + SEQ
PAIRS = BATCH // 2
GP = GB // 2
QUAD = HALF // HEAD_DIM
HEAD_PAIRS = HEADS // 2
MIX_TILES = (0, 2, 5, 7, TILES)
MIXES = len(MIX_TILES) - 1
MIX_MAX = max(b - a for a, b in zip(MIX_TILES, MIX_TILES[1:]))
CONSTS = P + SEQ + QUAD
PIX_RAW = 4
W_TOK_PARTS = 3
HI, LO = 0, 1
MIX_RING = 4
PASSES = ((HI, LO), (LO, HI), (HI, HI))

INPUTS = ["patches", "w_tok", "w_k", "w_q", "w_v", "w_o", "w_fk", "w_r", "w_fv",
          "b_tok", "b_o", "columns", "consts"]
WK, WQ, WV, WO, WFK, WR, WFV = range(7)
W_ORDER = (WV, WK, WQ, WO, WFK, WR, WFV)

def pieces():
    groups = [(g, c) for g in range(GROUPS) for c in range(FC)]
    tiles, pairs = [(t,) for t in range(TILES)], [(i,) for i in range(PAIRS)]
    mixes = [(u, n) for u in range(MIXES) for n in range(2)]
    every = {kind: tiles for kind in ("embed", "t1", "h1", "stats1", "moments1", "norm1", "y1", "rstd1", "residual",
                                      "o", "rstd2", "norm2", "t2", "r", "fv")}
    every |= {kind: pairs for kind in ("exp", "sums", "divide", "transpose", "probs", "attend", "attention", "vt")}
    every |= {kind: groups for kind in ("k", "q", "v")}
    every |= {kind: mixes for kind in ("scale", "sum", "high", "low", "fk")}
    every |= {kind: [(i, half) for i in range(PAIRS) for half in range(2)] for kind in ("score", "scores")}
    return every | {"start": [()], "constants": [()], "zero": [()], "pixels": tiles[1:],
                    "weight": [(n,) for n in range(len(W_ORDER))]}


PLAN = {
    "scalar": {
        "start": [0],
        "pixels": [1, 3, 4, 6, 10, 13, 18, 21],
        "weight": [2, 7, 9, 11, 14, 16, 17],
        "y1": [5, 8, 12, 15, 19, 23, 28, 31, 32],
        "probs": [43, 50, 56, 62, 66, 71, 80, 87, 96, 97, 103, 110, 116, 126, 127, 136],
        "attention": [51, 55, 60, 67, 72, 81, 84, 95, 101, 104, 108, 117, 123, 130, 134, 137],
        "exp": [38, 39, 45, 46, 57, 58, 65, 70, 77, 83, 94, 99, 106, 107, 114, 125],
        "k": [20, 25, 37, 42, 54, 59, 74, 85],
        "q": [27, 29, 41, 44, 63, 64, 89, 90],
        "v": [22, 24, 34, 36, 52, 53, 75, 76],
        "vt": [26, 30, 33, 35, 40, 47, 48, 49, 61, 68, 69, 73, 86, 91, 93, 100],
        "t2": [78, 79, 102, 105, 112, 120, 132, 141, 143],
        "scale": [82, 88, 115, 119, 133, 135, 145, 146],
        "high": [92, 98, 121, 122, 139, 140, 147, 149],
        "fk": [109, 111, 124, 128, 142, 144, 151, 152],
        "r": [113, 118, 129, 131, 138, 148, 150, 153, 154],
    },
    "gpsimd": {
        "rstd1": [0, 1, 2, 4, 7, 9, 13, 14, 17],
        "weight": [3, 5, 6, 8, 10, 11, 12],
        "zero": [20],
        "divide": [21, 26, 27, 28, 31, 32, 35, 38, 39, 40, 46, 48, 51, 53, 54, 56],
        "residual": [18, 19, 24, 25, 30, 34, 43, 44, 49],
        "k": [15, 16, 22, 23, 29, 33, 41, 45],
        "rstd2": [36, 37, 42, 47, 50, 52, 55, 57, 58],
    },
    "vector": {
        "start": [0],
        "pixels": [1, 5, 10, 16, 22, 27, 34, 40],
        "h1": [2, 6, 12, 18, 23, 29, 36, 42, 52],
        "norm1": [7, 11, 17, 24, 31, 35, 44, 51, 56],
        "stats1": [3, 8, 13, 20, 25, 30, 37, 45, 53],
        "y1": [14, 19, 26, 33, 39, 46, 50, 57, 68],
        "moments1": [4, 9, 15, 21, 28, 32, 38, 47, 54],
        "constants": [41],
        "scores": [60, 61, 62, 64, 67, 70, 73, 74, 79, 80, 83, 85, 89, 91, 94, 98, 102, 106, 109, 111, 116,
            118, 123, 126, 130, 133, 137, 141, 145, 148, 153, 154],
        "attention": [78, 84, 88, 96, 104, 110, 117, 124, 131, 138, 146, 155, 162, 167, 169, 173],
        "sums": [66, 71, 75, 81, 86, 92, 99, 105, 114, 120, 128, 136, 142, 149, 156, 165],
        "k": [43, 48, 63, 69, 82, 87, 108, 115],
        "vt": [49, 55, 58, 59, 65, 72, 76, 77, 90, 93, 95, 100, 113, 119, 125, 129],
        "o": [97, 101, 121, 127, 134, 150, 164, 171, 175],
        "norm2": [103, 107, 132, 135, 143, 152, 166, 176, 180],
        "sum": [112, 122, 151, 158, 170, 174, 184, 185],
        "low": [139, 140, 159, 161, 177, 178, 186, 187],
        "fk": [144, 147, 163, 168, 182, 183, 189, 190],
        "fv": [157, 160, 172, 179, 181, 188, 191, 192, 193],
    },
    "tensor": {
        "embed": [0, 1, 2, 4, 6, 8, 10, 16, 21],
        "t1": [3, 5, 7, 9, 12, 15, 20, 24, 27],
        "score": [28, 31, 32, 35, 38, 39, 43, 45, 49, 50, 55, 57, 63, 64, 67, 72, 77, 79, 86, 88, 93, 94,
            102, 103, 107, 108, 114, 115, 120, 123, 127, 129],
        "attend": [47, 56, 60, 68, 75, 84, 91, 99, 106, 111, 116, 128, 131, 139, 144, 148],
        "transpose": [41, 48, 54, 61, 65, 76, 82, 90, 98, 105, 110, 118, 124, 134, 138, 143],
        "k": [13, 17, 33, 37, 51, 59, 78, 89],
        "q": [19, 22, 34, 40, 62, 66, 92, 95],
        "v": [11, 14, 29, 30, 52, 53, 80, 81],
        "vt": [18, 23, 25, 26, 36, 42, 44, 46, 58, 69, 70, 73, 87, 96, 100, 101],
        "o": [71, 74, 97, 104, 109, 125, 137, 147, 149],
        "t2": [83, 85, 112, 113, 119, 132, 141, 153, 155],
        "fk": [117, 121, 135, 136, 152, 154, 160, 161],
        "r": [122, 130, 140, 142, 145, 156, 157, 162, 163],
        "fv": [126, 133, 146, 150, 151, 158, 159, 164, 165],
    },
}


def order(engine):
    timed = [(time, at, n, (kind, *which)) for at, (kind, times) in enumerate(PLAN[engine].items())
             for n, (which, time) in enumerate(zip(pieces()[kind], times, strict=True))]
    return [piece for *_, piece in sorted(timed)]



def vit_tower(nc, patches, w_tok, w_k, w_q, w_v, w_o, w_fk, w_r, w_fv,
              b_tok, b_o, columns, consts, out):
    f32, f32r, bf16 = mybir.dt.float32, mybir.dt.float32r, mybir.dt.bfloat16
    ALU, ACT, AX = mybir.AluOpType, mybir.ActivationFunctionType, mybir.AxisListType

    ctx = ExitStack()
    with ctx:
        def sb(name, shape, dt=f32, scope=ctx):
            return scope.enter_context(nc.sbuf_tensor(name, shape, dt))

        def sem(name):
            return ctx.enter_context(nc.semaphore(name))

        w = sb("w", [P, 7, 2, FC, DIM], f32r)
        o_bias = sb("o_bias", [P, DIM])
        cols = sb("cols", [P, 5, FC])
        bq, bk, bv, mu = cols[:, 0, :], cols[:, 1, :], cols[:, 2, :], cols[:, 3:5, :]
        one_less_mu = sb("one_less_mu", [P, 2, FC])
        const = sb("const", [P, CONSTS])
        ident = const[:, 0:P]
        causal = const[:, P:P + SEQ]
        head_mask = const[:, P + SEQ:CONSTS]
        ident_bf = sb("ident_bf", [P, P], bf16)
        causal_bf = sb("causal_bf", [P, GB, SEQ], bf16)
        power = sb("power", [P, 1])
        h = sb("h", [P, TILES, DIM])
        stats = sb("stats", [P, 2, TILES, 6])
        moments = sb("moments", [P, 2, TILES, 2])
        var_eps = sb("var_eps", [P, 2, TILES])
        rstd = sb("rstd", [P, 2, TILES])
        normed = sb("normed", [P, 2, DIM])
        y1 = sb("y1", [P, 2, FC, TOKENS], f32r)
        y2 = sb("y2", [P, FC, TOKENS])
        attn = sb("attn", [P, 2, FC, TOKENS], f32r)
        qT = sb("qT", [P, 2, FC, 2, GROUP])
        k_raw = sb("k_raw", [P, FC, GROUP])
        km = sb("km", [P, 2, FC, QUAD, GROUP])
        vT = sb("vT", [P, FC, GB, 2, HALF])
        vb = sb("vb", [P, 2, GB, HEAD_PAIRS, 2 * HEAD_DIM])
        with ExitStack() as early:
            w_raw = sb("w_raw", [P, 7, FC, DIM], scope=early)
        diff = sb("diff", [P, 2, HEADS, SEQ])
        probs = sb("probs", [P, 3, HEADS, HALF])
        row_max = sb("row_max", [P, 2, HEADS])
        row_sum = sb("row_sum", [P, 2, HEADS])
        row_inv = sb("row_inv", [P, 2, HEADS])
        pT = sb("pT", [P, 2, HEAD_PAIRS, 2, SEQ])
        with ExitStack() as early:
            tok_bias = sb("tok_bias", [P, DIM], scope=early)
            tok_w_raw = sb("tok_w_raw", [P, PC, DIM], scope=early)
            tok_w = sb("tok_w", [P, 2, PC, DIM], f32r, scope=early)
            pix_raw = sb("pix_raw", [P, PIX_RAW, PC, P], scope=early)
            pix = sb("pix", [P, 2, 2, PC, P], f32r, scope=early)
        mix_sum = sb("mix_sum", [P, MIX_RING, MIX_MAX * P])
        mixed = sb("mixed", [P, 2, 2, 2, FC, MIX_MAX * P], f32r)
        relu = sb("relu", [P, FC, MIX_MAX * P])
        square = sb("square", [P, FC, MIX_MAX * P])
        keys_sq = sb("keys_sq", [P, 2, FC, MIX_MAX * P], f32r)
        gate = sb("gate", [P, MIX_MAX, DIM])

        bank = [ctx.enter_context(nc.psum_tensor(f"bank{i}", [P, 512], f32)) for i in range(8)]

        dma_pix = [sem(f"dma_pix{t}") for t in range(TILES)]
        dma_first = [sem(f"dma_first{n}") for n in range(W_TOK_PARTS)]
        dma_w = [sem(f"dma_w{n}") for n in range(7)]
        dma_wtok = [sem(f"dma_wtok{n}") for n in range(W_TOK_PARTS)]
        dma_const, dma_bias, dma_o_bias, dma_cols = sem("dma_const"), sem("dma_bias"), sem("dma_o_bias"), sem("dma_cols")
        probs_zeroed, bf_ready, less_ready, zeroed = (sem("probs_zeroed"), sem("bf_ready"), sem("less_ready"),
                                                      sem("zeroed"))
        first_hi, first_lo = sem("first_hi"), sem("first_lo")
        wtok_hi, wtok_lo, w_hi, w_lo = sem("wtok_hi"), sem("wtok_lo"), sem("w_hi"), sem("w_lo")
        pix_hi, pix_lo, embedded, h_ready = sem("pix_hi"), sem("pix_lo"), sem("embedded"), sem("h_ready")
        bn_done, stats_ready, eps_added, rstd_ready = sem("bn_done"), sem("stats_ready"), sem("eps_added"), sem("rstd_ready")
        normed_ready, norm_transposed = sem("normed_ready"), sem("norm_transposed")
        y1_hi, y1_lo, y2_ready, resid_ready = sem("y1_hi"), sem("y1_lo"), sem("y2_ready"), sem("resid_ready")
        q_done, k_done, v_done, vt_done = sem("q_done"), sem("k_done"), sem("v_done"), sem("vt_done")
        q_ready, k_raw_ready, k_ready, k_last_ready = sem("q_ready"), sem("k_raw_ready"), sem("k_ready"), sem("k_last_ready")
        vT_ready, v_even_ready, v_odd_ready = sem("vT_ready"), sem("v_even_ready"), sem("v_odd_ready")
        scored, max_ready, diff_ready = sem("scored"), sem("max_ready"), sem("diff_ready")
        exp_ready, sum_ready, inv_ready, probs_ready = sem("exp_ready"), sem("sum_ready"), sem("inv_ready"), sem("probs_ready")
        probs_transposed, pT_ready = sem("probs_transposed"), sem("pT_ready")
        attended, attn_hi, attn_lo, projected = sem("attended"), sem("attn_hi"), sem("attn_lo"), sem("projected")
        scaled, mix_ready, mixed_hi, mixed_lo = sem("scaled"), sem("mix_ready"), sem("mixed_hi"), sem("mixed_lo")
        fk_done, relu_ready, square_ready, keys_hi, keys_lo = (sem("fk_done"), sem("relu_ready"), sem("square_ready"),
                                                               sem("keys_hi"), sem("keys_lo"))
        r_done, gate_ready, fv_done, gated, final_ready = (sem("r_done"), sem("gate_ready"), sem("fv_done"),
                                                           sem("gated"), sem("final_ready"))
        stored = sem("stored")

        E_BANKS, S_BANKS, T_BANKS, O_BANK = (0, 1, 2), (0, 1), (4, 5), 3

        dense, turn, late = {}, 0, False
        for piece in order("tensor"):
            if piece[0] in ("k", "q", "v", "vt", "o", "t2", "fk", "r", "fv"):
                dense[piece] = bank[(2, 6, 7, 0, 1, 3, 4, 5)[turn % (8 if late else 3)]]
                turn += 1
            if piece == ("attend", PAIRS - 1):
                turn, late = 3 if turn % 3 == 0 else 3 + turn % 3, True

        def mix_tokens(u):
            return MIX_TILES[u] * P, MIX_TILES[u + 1] * P

        def pair_place(p):
            half, chunk, m = p // 4, (p // 2) % 2, p % 2
            return chunk, (half * 2 + m) * 32, chunk * 4 + half * 2 + m

        def value_heads(n, odd):
            b = dense["vt", n][odd * HALF:(odd + 1) * HALF, :]
            return b.rearrange("p (b h o d) -> p b h o d", b=2, o=2, d=HEAD_DIM)[:, :, :, odd]

        def value_slots(n, odd):
            rows = vb[odd * HALF:(odd + 1) * HALF, (n // GP) % 2, 2 * (n % GP):2 * (n % GP) + 2]
            return rows[:, :, :, odd * HEAD_DIM:(odd + 1) * HEAD_DIM]

        block = ctx.enter_context(nc.Block())

        @block.sync
        def _(sp):
            def load_pixels(t):
                if t >= PIX_RAW:
                    sp.wait_ge(*((pix_lo, t - PIX_RAW) if t > PIX_RAW else (first_lo, W_TOK_PARTS)))
                sp.dma_start(pix_raw[:, t % PIX_RAW], patches[t]).then_inc(dma_pix[t], 16)

            def load_weight(n):
                sp.dma_start(w_raw[:, n], (w_k, w_q, w_v, w_o, w_fk, w_r, w_fv)[n]).then_inc(dma_w[n], 16)

            part = PC // W_TOK_PARTS
            for n in range(W_TOK_PARTS):
                sp.dma_start(tok_w_raw[:, n * part:(n + 1) * part], w_tok[:, n * part:(n + 1) * part]
                             ).then_inc(dma_wtok[n], 16)
                sp.dma_start(pix_raw[:, 0, n * part:(n + 1) * part], patches[0][:, n * part:(n + 1) * part]
                             ).then_inc(dma_first[n], 16)
            for t in range(1, PIX_RAW):
                load_pixels(t)
                if t == 1:
                    sp.dma_start(tok_bias[:], b_tok.to_broadcast([P, DIM])).then_inc(dma_bias, 16)
                    sp.dma_start(const[:], consts).then_inc(dma_const, 16)
                load_weight((None, WV, WK, WQ)[t])
            sp.dma_start(cols[:], columns).then_inc(dma_cols, 16)
            for t in range(PIX_RAW, TILES):
                load_pixels(t)
                if t - PIX_RAW < 4:
                    load_weight(WO + t - PIX_RAW)
            sp.dma_start(o_bias[:], b_o.to_broadcast([P, DIM])).then_inc(dma_o_bias, 16)
            for t in range(TILES):
                sp.wait_ge(final_ready, t + 1)
                sp.dma_start(out[t * P:(t + 1) * P, :], h[:, t]).then_inc(stored, 16)
            sp.wait_ge(stored, 16 * TILES)

        @block.scalar
        def _(act):
            def weight_hi(n):
                n = W_ORDER[n]
                act.wait_ge(dma_w[n], 16)
                nc.scalar.activation(w[:, n, HI], w_raw[:, n], ACT.Copy).then_inc(w_hi, 1)

            def pixels_hi(t):
                act.wait_ge(dma_pix[t], 16)
                if t >= 2:
                    act.wait_ge(embedded, t - 1)
                nc.scalar.activation(pix[:, t % 2, HI], pix_raw[:, t % PIX_RAW], ACT.Copy).then_inc(pix_hi, 1)

            def y1_high(t):
                act.wait_ge(norm_transposed, t + 1)
                nc.scalar.activation(y1[:, HI, :, t * P:(t + 1) * P],
                                     bank[T_BANKS[t % 2]][:, 0:DIM].rearrange("p (c n) -> p c n", c=FC),
                                     ACT.Copy).then_inc(y1_hi, 1)

            def exponentials(i):
                act.wait_ge(diff_ready, 2 * i + 2)
                if i == 0:
                    act.wait_ge(probs_zeroed, 1)
                if i >= 3:
                    act.wait_ge(probs_transposed, 2 * (i - 2))
                nc.scalar.activation(probs[:, i % 3, :, 0:SEQ], diff[:, i % 2], ACT.Exp,
                                     scale=HEAD_DIM ** -0.5).then_inc(exp_ready, 1)

            def probs_out(i):
                for part in range(2):
                    act.wait_ge(probs_transposed, 2 * i + part + 1)
                    if i >= 2:
                        act.wait_ge(attended, i - 1)
                    nc.scalar.activation(pT[:, i % 2, 4 * part:4 * part + 4],
                                         bank[T_BANKS[part]][:, :].rearrange("p (h b q) -> p h b q", h=4, b=2)
                                         [:, :, :, 0:SEQ], ACT.Copy).then_inc(pT_ready, 1)

            def attention_high(i):
                act.wait_ge(attended, i + 1)
                nc.scalar.activation(attn[:, HI, :, i * 2 * SEQ:(i + 1) * 2 * SEQ],
                                     bank[O_BANK][:, 0:FC * 2 * SEQ].rearrange("p (c n) -> p c n", c=FC),
                                     ACT.Copy).then_inc(attn_hi, 1)

            def start():
                part = PC // W_TOK_PARTS
                for n in range(W_TOK_PARTS):
                    act.wait_ge(dma_wtok[n], 16)
                    nc.scalar.activation(tok_w[:, HI, n * part:(n + 1) * part],
                                         tok_w_raw[:, n * part:(n + 1) * part], ACT.Copy).then_inc(wtok_hi, 1)
                    act.wait_ge(dma_first[n], 16)
                    nc.scalar.activation(pix[:, 0, HI, n * part:(n + 1) * part],
                                         pix_raw[:, 0, n * part:(n + 1) * part], ACT.Copy).then_inc(first_hi, 1)

            for kind, *a in order("scalar"):
                if kind == "start":
                    start()
                if kind == "pixels":
                    pixels_hi(*a)
                if kind == "weight":
                    weight_hi(*a)
                if kind == "y1":
                    y1_high(*a)
                if kind == "exp":
                    exponentials(*a)
                if kind == "probs":
                    probs_out(*a)
                if kind == "attention":
                    attention_high(*a)
                if kind in ("k", "q", "v") and a == [0, 0]:
                    act.wait_ge(dma_cols, 16)
                    act.wait_ge(zeroed, 4)
                if kind == "k":
                    g, c = a
                    act.wait_ge(k_done, FC * g + c + 1)
                    if g:
                        act.wait_ge(k_ready, FC * (g - 1) + c + 1)
                        act.wait_ge(k_last_ready, FC * (g - 1) + c + 1)
                    nc.scalar.activation(k_raw[:, c], dense["k", g, c][:, 0:GROUP], ACT.Identity,
                                         bias=bk[:, c:c + 1]).then_inc(k_raw_ready, 1)
                if kind == "q":
                    g, c = a
                    act.wait_ge(q_done, FC * g + c + 1)
                    if g >= 2:
                        act.wait_ge(scored, 2 * GP * (g - 1))
                    for half in range(2):
                        rows = slice(half * HALF, (half + 1) * HALF)
                        last = nc.scalar.activation(qT[rows, g % 2, c, half], dense["q", g, c][rows, 0:GROUP],
                                                    ACT.Identity, bias=bq[rows, c:c + 1])
                    last.then_inc(q_ready, 1)
                if kind == "v":
                    g, c = a
                    act.wait_ge(v_done, FC * g + c + 1)
                    if g:
                        act.wait_ge(vt_done, GP * g)
                    nc.scalar.activation(vT[:, c, :, :, 0:SEQ],
                                         dense["v", g, c][:, 0:GROUP].rearrange("p (b k) -> p b k", b=GB)
                                         .unsqueeze(2).to_broadcast([P, GB, 2, SEQ]),
                                         ACT.Identity, bias=bv[:, c:c + 1]).then_inc(vT_ready, 1)
                if kind == "vt":
                    n, = a
                    act.wait_ge(vt_done, n + 1)
                    if n >= 2 * GP:
                        act.wait_ge(attended, n - 2 * GP + 1)
                    nc.scalar.activation(value_slots(n, 1), value_heads(n, 1), ACT.Copy).then_inc(v_odd_ready, 1)
                if kind == "t2":
                    t, = a
                    act.wait_ge(norm_transposed, TILES + t + 1)
                    nc.scalar.activation(y2[:, :, t * P:(t + 1) * P],
                                         dense["t2", t][:, 0:DIM].rearrange("p (c n) -> p c n", c=FC),
                                         ACT.Copy).then_inc(y2_ready, 1)
                if kind == "scale":
                    u, which = a
                    lo, hi = mix_tokens(u)
                    act.wait_ge(y2_ready, MIX_TILES[u + 1])
                    for c in range(FC):
                        n = 4 * u + FC * which + c
                        if n >= MIX_RING:
                            act.wait_ge(mixed_lo, n - MIX_RING + 1)
                        nc.scalar.activation(mix_sum[:, n % MIX_RING, 0:hi - lo], y2[:, c, lo:hi], ACT.Copy,
                                             scale=mu[:, which, c:c + 1]).then_inc(scaled, 1)
                if kind == "high":
                    u, which = a
                    lo, hi = mix_tokens(u)
                    if u >= 2:
                        act.wait_ge(*((fk_done, FC * (u - 1)), (r_done, MIX_TILES[u - 1]))[which])
                    for c in range(FC):
                        n = 4 * u + FC * which + c
                        act.wait_ge(mix_ready, n + 1)
                        nc.scalar.activation(mixed[:, u % 2, which, HI, c, 0:hi - lo], mix_sum[:, n % MIX_RING, 0:hi - lo],
                                             ACT.Copy).then_inc(mixed_hi, 1)
                if kind == "fk":
                    u, c = a
                    n = FC * u + c
                    lo, hi = mix_tokens(u)
                    act.wait_ge(fk_done, n + 1)
                    if u:
                        act.wait_ge(square_ready, n - FC + 1)
                        act.wait_ge(fv_done, MIX_TILES[u])
                    nc.scalar.activation(relu[:, c, 0:hi - lo], dense["fk", u, c][:, 0:hi - lo], ACT.Relu
                                         ).then_inc(relu_ready, 1)
                    act.wait_ge(relu_ready, n + 1)
                    nc.scalar.activation(keys_sq[:, HI, c, 0:hi - lo], relu[:, c, 0:hi - lo], ACT.Square).then_inc(keys_hi, 1)
                if kind == "r":
                    t, = a
                    act.wait_ge(r_done, t + 1)
                    if t >= MIX_MAX:
                        act.wait_ge(final_ready, t - MIX_MAX + 1)
                    nc.scalar.activation(gate[:, t % MIX_MAX], dense["r", t][:, 0:DIM], ACT.Tanh,
                                         scale=0.5).then_inc(gate_ready, 1)

        @block.gpsimd
        def _(pool):
            nc.gpsimd.memset(power[:], -0.5).then_inc(zeroed, 1)
            nc.gpsimd.memset(vT[:, :, :, :, SEQ:].rearrange("p c b o k -> p (c b o) k"), 0.0).then_inc(zeroed, 1)

            nc.gpsimd.memset(qT[:], 0.0).then_inc(zeroed, 1)
            nc.gpsimd.memset(vb[:], 0.0).then_inc(zeroed, 1)

            def weight_lo(n):
                pool.wait_ge(w_hi, n + 1)
                n = W_ORDER[n]
                nc.gpsimd.tensor_tensor(w[:, n, LO], w_raw[:, n], w[:, n, HI].bitcast(f32),
                                        ALU.subtract).then_inc(w_lo, 1)

            def rstds(which, t):
                n = which * TILES + t
                pool.wait_ge(stats_ready, n + 1)
                nc.gpsimd.tensor_scalar(var_eps[:, which, t:t + 1], moments[:, which, t, 1:2], LN_EPS, None,
                                        ALU.add).then_inc(eps_added, 1)
                pool.wait_ge(eps_added, n + 1)
                nc.gpsimd.tensor_tensor(rstd[:, which, t:t + 1], var_eps[:, which, t:t + 1], power[:],
                                        ALU.pow).then_inc(rstd_ready, 1)

            pool.wait_ge(zeroed, 2)
            for kind, *a in order("gpsimd"):
                if kind == "weight":
                    weight_lo(*a)
                if kind == "rstd1":
                    rstds(0, *a)
                if kind == "rstd2":
                    rstds(1, *a)
                if kind == "zero":
                    pool.wait_ge(w_lo, 7)
                    nc.gpsimd.memset(probs[:, :, :, SEQ:].rearrange("p r s k -> p (r s) k"), 0.0
                                     ).then_inc(probs_zeroed, 1)
                if kind == "divide":
                    i, = a
                    pool.wait_ge(inv_ready, i + 1)
                    nc.gpsimd.tensor_tensor(probs[:, i % 3, :, 0:SEQ], probs[:, i % 3, :, 0:SEQ],
                                            row_inv[:, i % 2].unsqueeze(2).to_broadcast([P, HEADS, SEQ]),
                                            ALU.mult).then_inc(probs_ready, 1)
                if kind == "residual":
                    t, = a
                    if t == 0:
                        pool.wait_ge(dma_o_bias, 16)
                    pool.wait_ge(normed_ready, t + 1)
                    nc.gpsimd.tensor_tensor(h[:, t], h[:, t], o_bias[:], ALU.add).then_inc(resid_ready, 1)
                if kind == "k":
                    g, c = a
                    if g == 0 and c == 0:
                        pool.wait_ge(dma_const, 16)
                    pool.wait_ge(k_raw_ready, FC * g + c + 1)
                    if g >= 2:
                        pool.wait_ge(scored, 2 * GP * (g - 1))
                    nc.gpsimd.tensor_scalar(km[:, g % 2, c, QUAD - 1], k_raw[:, c], head_mask[:, QUAD - 1:QUAD], 0.0,
                                            ALU.mult, ALU.add).then_inc(k_last_ready, 1)

        @block.vector
        def _(dve):
            def pixels_lo(t):
                dve.wait_ge(pix_hi, t)
                nc.vector.tensor_tensor(pix[:, t % 2, LO], pix_raw[:, t % PIX_RAW], pix[:, t % 2, HI].bitcast(f32),
                                        ALU.subtract).then_inc(pix_lo, 1)

            def tile_stats(which, t):
                n = which * TILES + t
                dve.wait_ge(h_ready, n + 1)
                nc.vector.bn_stats(stats[:, which, t], h[:, t]).then_inc(bn_done, 1)

            def tile_moments(which, t):
                n = which * TILES + t
                dve.wait_ge(bn_done, n + 1)
                nc.vector.bn_aggr(moments[:, which, t], stats[:, which, t]).then_inc(stats_ready, 1)

            def normalise(which, t):
                n = which * TILES + t
                dve.wait_ge(rstd_ready, n + 1)
                if n >= 2:
                    dve.wait_ge(norm_transposed, n - 1)
                nc.vector.tensor_scalar(normed[:, n % 2], h[:, t], moments[:, which, t, 0:1],
                                        rstd[:, which, t:t + 1], ALU.subtract, ALU.mult).then_inc(normed_ready, 1)

            def y1_low(t):
                dve.wait_ge(y1_hi, t + 1)
                tokens = slice(t * P, (t + 1) * P)
                nc.vector.tensor_tensor(y1[:, LO, :, tokens],
                                        bank[T_BANKS[t % 2]][:, 0:DIM].rearrange("p (c n) -> p c n", c=FC),
                                        y1[:, HI, :, tokens].bitcast(f32), ALU.subtract).then_inc(y1_lo, 1)

            def softmax_scores(i, half):
                n = 2 * i + half
                scores = bank[S_BANKS[half]][:, 0:8 * SEQ].rearrange("p (s k) -> p s k", k=SEQ)
                heads = slice(8 * half, 8 * half + 8)
                dve.wait_ge(scored, n + 1)
                nc.vector.tensor_reduce(row_max[:, i % 2, heads], scores, AX.X, ALU.max).then_inc(max_ready, 1)
                dve.wait_ge(max_ready, n + 1)
                if i >= 2:
                    dve.wait_ge(exp_ready, i - 1)
                nc.vector.tensor_tensor(diff[:, i % 2, heads], scores,
                                        row_max[:, i % 2, heads].unsqueeze(2).to_broadcast([P, 8, SEQ]),
                                        ALU.subtract).then_inc(diff_ready, 1)

            def softmax_sums(i):
                dve.wait_ge(exp_ready, i + 1)
                nc.vector.tensor_reduce(row_sum[:, i % 2], probs[:, i % 3, :, 0:SEQ], AX.X,
                                        ALU.add).then_inc(sum_ready, 1)
                dve.wait_ge(sum_ready, i + 1)
                if i >= 2:
                    dve.wait_ge(probs_ready, i - 1)
                nc.vector.reciprocal(row_inv[:, i % 2], row_sum[:, i % 2]).then_inc(inv_ready, 1)

            def attention_low(i):
                dve.wait_ge(attn_hi, i + 1)
                tokens = slice(i * 2 * SEQ, (i + 1) * 2 * SEQ)
                nc.vector.tensor_tensor(attn[:, LO, :, tokens],
                                        bank[O_BANK][:, 0:FC * 2 * SEQ].rearrange("p (c n) -> p c n", c=FC),
                                        attn[:, HI, :, tokens].bitcast(f32), ALU.subtract).then_inc(attn_lo, 1)

            def shifted(u):
                (at, end), runs = mix_tokens(u), []
                while at < end:
                    q = at % SEQ
                    if q == 0 and end - at >= SEQ:
                        n = (end - at) // SEQ
                        runs.append((at + 1, n, SEQ - 1))
                        at += n * SEQ
                    else:
                        upto = min(end, at - q + SEQ)
                        at += q == 0
                        runs.append((at, 1, upto - at))
                        at = upto
                return runs

            def start():
                part = PC // W_TOK_PARTS
                for n in range(W_TOK_PARTS):
                    dve.wait_ge(wtok_hi, n + 1)
                    chunks = slice(n * part, (n + 1) * part)
                    nc.vector.tensor_tensor(tok_w[:, LO, chunks], tok_w_raw[:, chunks],
                                            tok_w[:, HI, chunks].bitcast(f32), ALU.subtract).then_inc(wtok_lo, 1)
                    dve.wait_ge(first_hi, n + 1)
                    nc.vector.tensor_tensor(pix[:, 0, LO, chunks], pix_raw[:, 0, chunks],
                                            pix[:, 0, HI, chunks].bitcast(f32), ALU.subtract).then_inc(first_lo, 1)

            for kind, *a in order("vector"):
                if kind == "start":
                    start()
                if kind == "pixels":
                    pixels_lo(*a)
                if kind == "h1":
                    t, = a
                    if t == 0:
                        dve.wait_ge(dma_bias, 16)
                    dve.wait_ge(embedded, t + 1)
                    nc.vector.tensor_tensor(h[:, t], bank[E_BANKS[t % 3]][:, 0:DIM], tok_bias[:],
                                            ALU.add).then_inc(h_ready, 1)
                if kind == "stats1":
                    tile_stats(0, *a)
                if kind == "moments1":
                    tile_moments(0, *a)
                if kind == "norm1":
                    normalise(0, *a)
                if kind == "y1":
                    y1_low(*a)
                if kind == "constants":
                    dve.wait_ge(dma_const, 16)
                    dve.wait_ge(dma_cols, 16)
                    nc.vector.tensor_copy(ident_bf[:], ident).then_inc(bf_ready, 1)
                    nc.vector.tensor_copy(causal_bf[:], causal.unsqueeze(1).to_broadcast([P, GB, SEQ])
                                          ).then_inc(bf_ready, 1)
                    nc.vector.tensor_scalar(one_less_mu[:], mu, -1.0, 1.0, ALU.mult, ALU.add).then_inc(less_ready, 1)
                if kind == "scores":
                    softmax_scores(*a)
                if kind == "sums":
                    softmax_sums(*a)
                if kind == "attention":
                    attention_low(*a)
                if kind == "k":
                    g, c = a
                    dve.wait_ge(k_raw_ready, FC * g + c + 1)
                    if g >= 2:
                        dve.wait_ge(scored, 2 * GP * (g - 1))
                    for m in range(QUAD - 1):
                        last = nc.vector.tensor_scalar(km[:, g % 2, c, m], k_raw[:, c], head_mask[:, m:m + 1], None,
                                                       ALU.mult)
                    last.then_inc(k_ready, 1)
                if kind == "vt":
                    n, = a
                    dve.wait_ge(vt_done, n + 1)
                    if n >= 2 * GP:
                        dve.wait_ge(attended, n - 2 * GP + 1)
                    nc.vector.tensor_copy(value_slots(n, 0), value_heads(n, 0)).then_inc(v_even_ready, 1)
                if kind == "o":
                    t, = a
                    dve.wait_ge(projected, t + 1)
                    dve.wait_ge(resid_ready, t + 1)
                    nc.vector.tensor_tensor(h[:, t], dense["o", t][:, 0:DIM], h[:, t],
                                            ALU.add).then_inc(h_ready, 1)
                    tile_stats(1, t)
                    tile_moments(1, t)
                if kind == "norm2":
                    normalise(1, *a)
                if kind == "sum":
                    u, which = a
                    dve.wait_ge(less_ready, 1)
                    for c in range(FC):
                        n = 4 * u + FC * which + c
                        dve.wait_ge(scaled, n + 1)
                        for first, batches, length in shifted(u):
                            at = first - mix_tokens(u)[0]
                            if batches > 1:
                                here = mix_sum[:, n % MIX_RING, at - 1:at - 1 + batches * SEQ]
                                before = y2[:, c, first - 1:first - 1 + batches * SEQ]
                                here = here.rearrange("p (b q) -> p b q", q=SEQ)[:, :, 1:]
                                before = before.rearrange("p (b q) -> p b q", q=SEQ)[:, :, 0:SEQ - 1]
                            else:
                                here = mix_sum[:, n % MIX_RING, at:at + length]
                                before = y2[:, c, first - 1:first - 1 + length]
                            last = nc.vector.scalar_tensor_tensor(here, before, one_less_mu[:, which, c:c + 1], here,
                                                                  ALU.mult, ALU.add)
                        last.then_inc(mix_ready, 1)
                if kind == "low":
                    u, which = a
                    lo, hi = mix_tokens(u)
                    for c in range(FC):
                        n = 4 * u + FC * which + c
                        dve.wait_ge(mixed_hi, n + 1)
                        nc.vector.tensor_tensor(mixed[:, u % 2, which, LO, c, 0:hi - lo], mix_sum[:, n % MIX_RING, 0:hi - lo],
                                                mixed[:, u % 2, which, HI, c, 0:hi - lo].bitcast(f32),
                                                ALU.subtract).then_inc(mixed_lo, 1)
                if kind == "fk":
                    u, c = a
                    n = FC * u + c
                    lo, hi = mix_tokens(u)
                    now = slice(0, hi - lo)
                    dve.wait_ge(relu_ready, n + 1)
                    nc.vector.tensor_tensor(square[:, c, now], relu[:, c, now], relu[:, c, now],
                                            ALU.mult).then_inc(square_ready, 1)
                    dve.wait_ge(square_ready, n + 1)
                    dve.wait_ge(keys_hi, n + 1)
                    nc.vector.tensor_tensor(keys_sq[:, LO, c, now], square[:, c, now], keys_sq[:, HI, c, now].bitcast(f32),
                                            ALU.subtract).then_inc(keys_lo, 1)
                if kind == "fv":
                    t, = a
                    dve.wait_ge(fv_done, t + 1)
                    dve.wait_ge(gate_ready, t + 1)
                    nc.vector.scalar_tensor_tensor(gate[:, t % MIX_MAX], gate[:, t % MIX_MAX], 1.0,
                                                   dense["fv", t][:, 0:DIM],
                                                   ALU.add, ALU.mult).then_inc(gated, 1)
                    dve.wait_ge(gated, t + 1)
                    nc.vector.scalar_tensor_tensor(h[:, t], gate[:, t % MIX_MAX], 0.5, h[:, t],
                                                   ALU.mult, ALU.add).then_inc(final_ready, 1)

        @block.tensor
        def _(pe):
            emptied = {b.name: () for b in bank}

            def claim(b, *reads):
                for semaphore, count in emptied[b.name]:
                    pe.wait_ge(semaphore, count)
                emptied[b.name] = reads

            def product(result, chunks, stationary, moving):
                for f in range(chunks):
                    for n, (a, b) in enumerate(PASSES):
                        last = nc.tensor.matmul(result, stationary(a, f), moving(b, f),
                                                start=(f == 0 and n == 0), stop=(f == chunks - 1 and n == 2))
                return last

            def embed(t):
                claim(bank[E_BANKS[t % 3]], (h_ready, t + 1))
                if t:
                    pe.wait_ge(pix_lo, t)
                part = PC // W_TOK_PARTS
                for c in range(PC):
                    if t == 0 and c % part == 0:
                        pe.wait_ge(wtok_lo, c // part + 1)
                        pe.wait_ge(first_lo, c // part + 1)
                    for n, (a, b) in enumerate(PASSES):
                        last = nc.tensor.matmul(bank[E_BANKS[t % 3]][:, 0:DIM], pix[:, t % 2, a, c], tok_w[:, b, c],
                                                start=(c == 0 and n == 0), stop=(c == PC - 1 and n == 2))
                last.then_inc(embedded, 1)

            def transpose_norm(which, t, b):
                n = which * TILES + t
                pe.wait_ge(normed_ready, n + 1)
                for c in range(FC):
                    last = nc.tensor.transpose(b[:, c * P:(c + 1) * P], normed[:, n % 2, c * P:(c + 1) * P], ident)
                last.then_inc(norm_transposed, 1)

            def score(i, half):
                n = 2 * i + half
                b = bank[S_BANKS[half]]
                g, first = i // GP, (i % GP) * 2
                pe.wait_ge(q_ready, FC * (g + 1))
                pe.wait_ge(k_ready, FC * (g + 1))
                pe.wait_ge(k_last_ready, FC * (g + 1))
                if n == 0:
                    pe.wait_ge(bf_ready, 2)
                claim(b, (diff_ready, n + 1))
                nc.tensor.matmul(b[:, 0:8 * SEQ], ident_bf[:], causal_bf[:].rearrange("p s k -> p (s k)"),
                                 start=True, stop=False, skip_group_check=True)
                for c in range(FC):
                    for e in range(2):
                        tok = slice((first + e) * SEQ, (first + e + 1) * SEQ)
                        last = nc.tensor.matmul(b[e * HALF:e * HALF + SEQ, c * 4 * SEQ:(c + 1) * 4 * SEQ],
                                                qT[:, g % 2, c, half, tok], km[:, g % 2, c, :, tok],
                                                start=False, stop=True, skip_group_check=True)
                last.then_inc(scored, 1)

            def transpose_probs(i):
                pe.wait_ge(probs_ready, i + 1)
                for part in range(2):
                    b = bank[T_BANKS[part]]
                    claim(b, (pT_ready, 2 * i + part + 1))
                    for p in range(4):
                        pair = probs[0:ROWS, i % 3, 8 * part + 2 * p:8 * part + 2 * p + 2]
                        last = nc.tensor.transpose(b[:, p * P:p * P + ROWS], pair.rearrange("p h k -> p (h k)"),
                                                   ident[0:ROWS, 0:ROWS])
                    last.then_inc(probs_transposed, 1)

            def attend(i):
                pe.wait_ge(pT_ready, 2 * i + 2)
                pe.wait_ge(v_even_ready, i + 1)
                pe.wait_ge(v_odd_ready, i + 1)
                claim(bank[O_BANK], (attn_lo, i + 1))
                for e in range(2):
                    for p in range(HEAD_PAIRS):
                        c, row, true_pair = pair_place(p)
                        last = nc.tensor.matmul(
                            bank[O_BANK][row:row + 32, (c * 2 + e) * SEQ:(c * 2 + e + 1) * SEQ],
                            vb[:, (i // GP) % 2, 2 * (i % GP) + e, true_pair], pT[:, i % 2, p, e], start=True, stop=True,
                            tile_position=(0, row), skip_group_check=True)
                last.then_inc(attended, 1)

            for kind, *a in order("tensor"):
                if kind == "embed":
                    embed(*a)
                if kind == "t1":
                    t, = a
                    if t == 0:
                        pe.wait_ge(dma_const, 16)
                    claim(bank[T_BANKS[t % 2]], (y1_lo, t + 1))
                    transpose_norm(0, t, bank[T_BANKS[t % 2]])
                if kind == "score":
                    score(*a)
                if kind == "attend":
                    attend(*a)
                if kind == "transpose":
                    transpose_probs(*a)
                b = dense.get((kind, *a))
                if kind in ("k", "q", "v"):
                    g, c = a
                    n, done, read = {"k": (WK, k_done, k_raw_ready), "q": (WQ, q_done, q_ready),
                                     "v": (WV, v_done, vT_ready)}[kind]
                    claim(b, (read, FC * g + c + 1))
                    pe.wait_ge(w_lo, W_ORDER.index(n) + 1)
                    pe.wait_ge(y1_lo, -(-(g + 1) * GROUP // P))
                    product(b[:, 0:GROUP], FC, lambda x, f: w[:, n, x, f, c * P:(c + 1) * P],
                            lambda x, f: y1[:, x, f, g * GROUP:(g + 1) * GROUP]).then_inc(done, 1)
                if kind == "vt":
                    n, = a
                    claim(b, (v_even_ready, n + 1), (v_odd_ready, n + 1))
                    pe.wait_ge(vT_ready, FC * (n // GP + 1))
                    for e in range(2):
                        for c in range(FC):
                            last = nc.tensor.transpose(b[:, (e * FC + c) * P:(e * FC + c + 1) * P],
                                                       vT[:, c, (2 * n + e) % GB].rearrange("p o k -> p (o k)"), ident)
                    last.then_inc(vt_done, 1)
                if kind == "o":
                    t, = a
                    claim(b, (h_ready, TILES + t + 1))
                    pe.wait_ge(w_lo, WO + 1)
                    pe.wait_ge(attn_lo, -(-(t + 1) * P // (2 * SEQ)))
                    product(b[:, 0:DIM], FC, lambda x, f: attn[:, x, f, t * P:(t + 1) * P],
                            lambda x, f: w[:, WO, x, f]).then_inc(projected, 1)
                if kind == "t2":
                    t, = a
                    claim(b, (y2_ready, t + 1))
                    transpose_norm(1, t, b)
                if kind == "fk":
                    u, c = a
                    claim(b, (relu_ready, FC * u + c + 1))
                    pe.wait_ge(mixed_lo, 4 * u + FC)
                    n = mix_tokens(u)[1] - mix_tokens(u)[0]
                    product(b[:, 0:n], FC, lambda x, f: w[:, WFK, x, f, c * P:(c + 1) * P],
                            lambda x, f: mixed[:, u % 2, 0, x, f, 0:n]).then_inc(fk_done, 1)
                if kind == "r":
                    t, = a
                    u = max(n for n in range(MIXES) if MIX_TILES[n] <= t)
                    at = (t - MIX_TILES[u]) * P
                    claim(b, (gate_ready, t + 1))
                    pe.wait_ge(mixed_lo, 4 * u + 2 * FC)
                    product(b[:, 0:DIM], FC, lambda x, f: mixed[:, u % 2, 1, x, f, at:at + P],
                            lambda x, f: w[:, WR, x, f]).then_inc(r_done, 1)
                if kind == "fv":
                    t, = a
                    u = max(n for n in range(MIXES) if MIX_TILES[n] <= t)
                    at = (t - MIX_TILES[u]) * P
                    claim(b, (gated, t + 1))
                    pe.wait_ge(keys_lo, FC * (u + 1))
                    product(b[:, 0:DIM], FC, lambda x, f: keys_sq[:, x, f, at:at + P],
                            lambda x, f: w[:, WFV, x, f]).then_inc(fv_done, 1)


def kernel(x, L0_tok_W, L0_tok_b, L0_attn_Wq, L0_attn_bq, L0_attn_Wk, L0_attn_bk, L0_attn_Wv, L0_attn_bv,
           L0_attn_Wo, L0_attn_bo, L0_ffn_W_r, L0_ffn_W_k, L0_ffn_W_v, L0_ffn_mu_r, L0_ffn_mu_k):
    import numpy as np
    import concourse.bacc as bacc
    from concourse.bass_utils import run_bass_kernel_spmd

    def weight(w, chunks):
        return np.ascontiguousarray(np.asarray(w).T.reshape(chunks, P, DIM).transpose(1, 0, 2))

    def column(v):
        return np.ascontiguousarray(np.asarray(v).reshape(FC, P).T)

    pixels = np.asarray(x).reshape(BATCH, CHANNELS, GRID, PATCH, GRID, PATCH).transpose(1, 3, 5, 0, 2, 4)
    pixels = pixels.reshape(PC, P, TILES, P).transpose(2, 1, 0, 3)

    row = np.arange(P)[:, None]
    blocked = (np.arange(SEQ)[None, :] > row % HALF) & (row % HALF < SEQ)
    consts = np.concatenate([np.eye(P), np.where(blocked, MASKED, 0.0),
                             row // HEAD_DIM % QUAD == np.arange(QUAD)[None, :]], axis=1).astype(np.float32)

    arrays = dict(zip(INPUTS, [
        np.ascontiguousarray(pixels), weight(L0_tok_W, PC),
        *(weight(w, FC) for w in (L0_attn_Wk, L0_attn_Wq, L0_attn_Wv, L0_attn_Wo, L0_ffn_W_k, L0_ffn_W_r, L0_ffn_W_v)),
        np.asarray(L0_tok_b).reshape(1, DIM), np.asarray(L0_attn_bo).reshape(1, DIM),
        np.ascontiguousarray(np.stack([column(v) for v in (L0_attn_bq, L0_attn_bk, L0_attn_bv, L0_ffn_mu_k,
                                                           L0_ffn_mu_r)], axis=1)), consts]))

    nc = bacc.Bacc("TRN2", target_bir_lowering=False, num_devices=1)
    args = [nc.dram_tensor(n, a.shape, mybir.dt.from_np(a.dtype), kind="ExternalInput").ap()
            for n, a in arrays.items()]
    out = nc.dram_tensor("out", (TOKENS, DIM), mybir.dt.float32, kind="ExternalOutput").ap()
    vit_tower(nc, *args, out)
    result = run_bass_kernel_spmd(nc, [arrays], core_ids=[0])
    return result.results[0]["out"].reshape(BATCH, SEQ, DIM)
```

```python
from contextlib import ExitStack

import concourse.bass as bass
from concourse import mybir

BATCH, CHANNELS, IMAGE, PATCH = 32, 3, 96, 16
GRID = IMAGE // PATCH
SEQ = GRID * GRID
TOKENS = BATCH * SEQ
PIXELS = CHANNELS * PATCH * PATCH
P = 128
DIM, HEADS = 256, 16
HEAD_DIM = DIM // HEADS
FC = DIM // P
PC = PIXELS // P
TILES = TOKENS // P
LN_EPS = 1e-5
MASKED = -1e38

GB = 8
GROUP = GB * SEQ
GROUPS = TOKENS // GROUP
HALF = P // 2
ROWS = HALF + SEQ
PAIRS = BATCH // 2
GP = GB // 2
QUAD = HALF // HEAD_DIM
HEAD_PAIRS = HEADS // 2
MIX_TILES = (0, 2, 5, 7, TILES)
MIXES = len(MIX_TILES) - 1
EARLY_OUT = 7
MIX_MAX = max(b - a for a, b in zip(MIX_TILES, MIX_TILES[1:]))
CONSTS = P + SEQ + QUAD
PIX_RAW = 3
PIX_SPLIT = 3
W_TOK_PARTS = 3
WARM_UP = 17
HI, LO = 0, 1
KEYS, GATE = 0, 1
PASSES = ((HI, LO), (LO, HI), (HI, HI))

INPUTS = ["patches", "w_tok", "w_k", "w_q", "w_v", "w_o", "w_fk", "w_r", "w_fv",
          "b_tok", "b_o", "columns", "consts"]
WK, WQ, WV, WO, WFK, WR, WFV = range(7)
W_ORDER = (WV, WK, WQ, WO, WFK, WR, WFV)

def pieces():
    groups = [(g, c) for g in range(GROUPS) for c in range(FC)]
    tiles, pairs = [(t,) for t in range(TILES)], [(i,) for i in range(PAIRS)]
    mixes = [(u, n) for u in range(MIXES) for n in range(2)]
    every = {kind: tiles for kind in ("embed", "t1", "h1", "stats1", "moments1", "norm1", "y1", "rstd1", "residual",
                                      "o", "rstd2", "norm2", "t2", "r", "fv")}
    every |= {kind: pairs for kind in ("exp", "sums", "divide", "transpose", "probs", "attend", "attention", "vt")}
    every |= {kind: groups for kind in ("k", "q", "v")}
    every |= {kind: mixes for kind in ("scale", "sum", "high", "fk")}
    every |= {kind: [(i, half) for i in range(PAIRS) for half in range(2)] for kind in ("score", "scores")}
    every["keys_low"] = every["gate_low"] = [(u,) for u in range(MIXES)]
    every["early_out"], every["weight_v"] = tiles[:EARLY_OUT], [()]
    return every | {"start": [()], "constants": [()], "zero": [()], "pixels": tiles[1:],
                    "weight": [(n,) for n in range(len(W_ORDER))]}


PLAN = {
    "scalar": {
        "start": [0],
        "pixels": [1, 2, 3, 5, 8, 9, 15, 17],
        "weight": [6, 10, 12, 13, 14, 16, 19],
        "y1": [4, 7, 11, 18, 20, 25, 26, 35, 38],
        "probs": [44, 50, 55, 59, 66, 74, 79, 86, 89, 97, 99, 108, 116, 123, 129, 133],
        "attention": [53, 57, 60, 68, 72, 75, 84, 91, 96, 102, 107, 113, 118, 127, 132, 136],
        "exp": [36, 39, 45, 49, 58, 63, 65, 71, 78, 82, 93, 98, 103, 105, 124, 125],
        "k": [23, 24, 37, 42, 51, 56, 76, 83],
        "q": [28, 29, 41, 43, 62, 67, 87, 95],
        "v": [21, 22, 32, 34, 52, 54, 70, 81],
        "vt": [27, 30, 31, 33, 40, 46, 47, 48, 61, 64, 69, 73, 90, 92, 104, 106],
        "t2": [77, 80, 100, 101, 110, 120, 130, 139, 144],
        "scale": [85, 88, 111, 115, 131, 137, 145, 146],
        "high": [94, 109, 119, 121, 135, 138, 148, 149],
        "fk": [112, 114, 126, 128, 142, 143, 151, 152],
        "r": [117, 122, 134, 140, 141, 147, 150, 153, 154],
    },
    "gpsimd": {
        "rstd1": [0, 1, 2, 3, 5, 10, 11, 13, 17],
        "weight": [4, 6, 7, 8, 12, 14, 19],
        "zero": [18],
        "divide": [20, 23, 25, 26, 33, 35, 36, 40, 43, 45, 47, 49, 51, 53, 56, 58],
        "residual": [9, 22, 27, 30, 31, 32, 34, 37, 42],
        "k": [15, 16, 21, 24, 28, 29, 41, 44],
        "rstd2": [38, 39, 46, 48, 50, 54, 57, 59, 63],
        "gate_low": [52, 55, 64, 66],
        "early_out": [60, 61, 62, 65, 67, 68, 69],
    },
    "vector": {
        "start": [0],
        "pixels": [1, 5, 10, 15, 22, 27, 35, 38],
        "h1": [2, 7, 12, 18, 23, 29, 34, 42, 50],
        "norm1": [6, 11, 20, 25, 28, 39, 43, 52, 56],
        "stats1": [3, 8, 14, 19, 24, 33, 36, 45, 51],
        "y1": [13, 16, 30, 32, 44, 48, 49, 59, 62],
        "moments1": [4, 9, 17, 21, 26, 37, 40, 46, 54],
        "constants": [31],
        "scores": [55, 57, 58, 61, 64, 66, 68, 69, 70, 72, 76, 77, 80, 83, 85, 89, 91, 96, 97, 100, 102,
            106, 111, 112, 115, 117, 122, 124, 128, 131, 137, 141],
        "attention": [75, 79, 82, 88, 92, 99, 105, 110, 116, 126, 129, 136, 140, 148, 152, 155],
        "sums": [60, 65, 71, 73, 78, 84, 87, 93, 101, 103, 114, 120, 127, 130, 144, 147],
        "k": [41, 47, 63, 67, 74, 81, 98, 109],
        "o": [86, 90, 108, 113, 121, 135, 146, 154, 160],
        "norm2": [94, 95, 118, 119, 125, 138, 149, 157, 162],
        "sum": [104, 107, 132, 139, 153, 156, 166, 167],
        "fk": [133, 134, 150, 151, 163, 164, 170, 171],
        "fv": [143, 145, 158, 161, 165, 169, 172, 173, 174],
        "keys_low": [123, 142, 159, 168],
        "weight_v": [53],
    },
    "tensor": {
        "embed": [0, 1, 2, 5, 6, 8, 10, 15, 20],
        "t1": [3, 4, 7, 9, 11, 18, 19, 23, 34],
        "score": [26, 30, 31, 33, 38, 39, 45, 47, 48, 50, 53, 58, 59, 64, 66, 68, 78, 79, 82, 86, 89, 92,
            99, 100, 105, 106, 108, 113, 117, 121, 126, 128],
        "attend": [46, 57, 63, 67, 77, 81, 90, 98, 103, 111, 118, 124, 130, 135, 142, 145],
        "transpose": [41, 49, 54, 61, 70, 73, 83, 91, 95, 104, 107, 116, 125, 129, 139, 143],
        "k": [14, 16, 32, 36, 52, 56, 80, 87],
        "q": [21, 22, 37, 40, 62, 71, 93, 102],
        "v": [12, 13, 28, 29, 51, 55, 74, 85],
        "vt": [17, 24, 25, 27, 35, 42, 43, 44, 60, 69, 72, 75, 94, 97, 114, 115],
        "o": [65, 76, 96, 101, 109, 123, 136, 144, 148],
        "t2": [84, 88, 110, 112, 119, 131, 140, 150, 155],
        "fk": [120, 122, 137, 138, 153, 154, 160, 161],
        "r": [127, 132, 141, 146, 152, 156, 157, 162, 163],
        "fv": [133, 134, 147, 149, 151, 158, 159, 164, 165],
    },
}


def order(engine):
    placed = {place: (kind, *which) for kind, places in PLAN[engine].items()
              for which, place in zip(pieces()[kind], places, strict=True)}
    return [placed[n] for n in range(len(placed))]


def vit_tower(nc, patches, w_tok, w_k, w_q, w_v, w_o, w_fk, w_r, w_fv,
              b_tok, b_o, columns, consts, out):
    f32, f32r, bf16 = mybir.dt.float32, mybir.dt.float32r, mybir.dt.bfloat16
    ALU, ACT, AX = mybir.AluOpType, mybir.ActivationFunctionType, mybir.AxisListType

    ctx = ExitStack()
    with ctx:
        def sb(name, shape, dt=f32, scope=ctx):
            return scope.enter_context(nc.sbuf_tensor(name, shape, dt))

        def sem(name):
            return ctx.enter_context(nc.semaphore(name))

        w = sb("w", [P, 7, 2, FC, DIM], f32r)
        o_bias = sb("o_bias", [P, DIM])
        cols = sb("cols", [P, 5, FC])
        bq, bk, bv, mu = cols[:, 0, :], cols[:, 1, :], cols[:, 2, :], cols[:, 3:5, :]
        one_less_mu = sb("one_less_mu", [P, 2, FC])
        const = sb("const", [P, CONSTS])
        ident = const[:, 0:P]
        causal = const[:, P:P + SEQ]
        head_mask = const[:, P + SEQ:CONSTS]
        ident_bf = sb("ident_bf", [P, P], bf16)
        causal_bf = sb("causal_bf", [P, GB, SEQ], bf16)
        power = sb("power", [P, 1])
        h = sb("h", [P, TILES, DIM])
        stats = sb("stats", [P, 2, TILES, 6])
        moments = sb("moments", [P, 2, TILES, 2])
        var_eps = sb("var_eps", [P, 2, TILES])
        rstd = sb("rstd", [P, 2, TILES])
        normed = sb("normed", [P, 2, DIM])
        y1 = sb("y1", [P, 2, FC, TOKENS], f32r)
        y2 = sb("y2", [P, FC, TOKENS])
        attn = sb("attn", [P, 2, FC, TOKENS], f32r)
        qT = sb("qT", [P, 2, FC, 2, GROUP])
        k_raw = sb("k_raw", [P, FC, GROUP])
        km = sb("km", [P, 2, FC, QUAD, GROUP])
        vT = sb("vT", [P, FC, GB, 2, HALF])
        vb = sb("vb", [P, 2, GB, HEAD_PAIRS, 2 * HEAD_DIM])
        with ExitStack() as early:
            w_raw = sb("w_raw", [P, 7, FC, DIM], scope=early)
            tok_bias = sb("tok_bias", [P, DIM], scope=early)
        diff = sb("diff", [P, 2, HEADS, SEQ])
        probs = sb("probs", [P, 3, HEADS, HALF])
        row_max = sb("row_max", [P, 2, HEADS])
        row_sum = sb("row_sum", [P, 2, HEADS])
        row_inv = sb("row_inv", [P, 2, HEADS])
        pT = sb("pT", [P, 2, HEAD_PAIRS, 2, SEQ])
        with ExitStack() as early:
            tok_w_raw = sb("tok_w_raw", [P, PC, DIM], scope=early)
            tok_w = sb("tok_w", [P, 2, PC, DIM], f32r, scope=early)
            pix_raw = sb("pix_raw", [P, PIX_RAW, PC, P], scope=early)
            pix = sb("pix", [P, PIX_SPLIT, 2, PC, P], f32r, scope=early)
        mix_sum = sb("mix_sum", [P, 2, FC, MIX_MAX * P])
        mixed = sb("mixed", [P, 2, 2, 2, FC, MIX_MAX * P], f32r)
        relu = sb("relu", [P, FC, MIX_MAX * P])
        square = sb("square", [P, FC, MIX_MAX * P])
        keys_sq = sb("keys_sq", [P, 2, FC, MIX_MAX * P], f32r)
        gate = sb("gate", [P, MIX_MAX, DIM])

        bank = [ctx.enter_context(nc.psum_tensor(f"bank{i}", [P, 512], f32)) for i in range(8)]

        dma_pix = [sem(f"dma_pix{t}") for t in range(TILES)]
        dma_first = [sem(f"dma_first{n}") for n in range(W_TOK_PARTS)]
        dma_w = [sem(f"dma_w{n}") for n in range(7)]
        dma_wtok = [sem(f"dma_wtok{n}") for n in range(W_TOK_PARTS)]
        dma_const, dma_bias, dma_o_bias, dma_cols = sem("dma_const"), sem("dma_bias"), sem("dma_o_bias"), sem("dma_cols")
        probs_zeroed, bf_ready, less_ready, zeroed = (sem("probs_zeroed"), sem("bf_ready"), sem("less_ready"),
                                                      sem("zeroed"))
        warm_ready, warmed = sem("warm_ready"), sem("warmed")
        first_hi, first_lo = sem("first_hi"), sem("first_lo")
        wtok_hi, wtok_lo, w_hi, w_lo = sem("wtok_hi"), sem("wtok_lo"), sem("w_hi"), sem("w_lo")
        pix_hi, pix_lo, embedded, h_ready = sem("pix_hi"), sem("pix_lo"), sem("embedded"), sem("h_ready")
        bn_done, stats_ready, eps_added, rstd_ready = sem("bn_done"), sem("stats_ready"), sem("eps_added"), sem("rstd_ready")
        normed_ready, norm_transposed = sem("normed_ready"), sem("norm_transposed")
        y1_hi, y1_lo, y2_ready, resid_ready = sem("y1_hi"), sem("y1_lo"), sem("y2_ready"), sem("resid_ready")
        q_done, k_done, v_done, vt_done = sem("q_done"), sem("k_done"), sem("v_done"), sem("vt_done")
        q_ready, k_raw_ready, k_ready, k_last_ready = sem("q_ready"), sem("k_raw_ready"), sem("k_ready"), sem("k_last_ready")
        vT_ready, v_even_ready, v_odd_ready = sem("vT_ready"), sem("v_even_ready"), sem("v_odd_ready")
        scored, max_ready, diff_ready = sem("scored"), sem("max_ready"), sem("diff_ready")
        exp_ready, sum_ready, inv_ready, probs_ready = sem("exp_ready"), sem("sum_ready"), sem("inv_ready"), sem("probs_ready")
        probs_transposed, pT_ready = sem("probs_transposed"), sem("pT_ready")
        attended, attn_hi, attn_lo, projected = sem("attended"), sem("attn_hi"), sem("attn_lo"), sem("projected")
        scaled, mix_ready, mixed_hi, mixed_lo = ([sem(f"{name}_{which}") for which in ("keys", "gate")]
                                                 for name in ("scaled", "mix_ready", "mixed_hi", "mixed_lo"))
        fk_done, relu_ready, square_ready, keys_hi, keys_lo = (sem("fk_done"), sem("relu_ready"), sem("square_ready"),
                                                               sem("keys_hi"), sem("keys_lo"))
        r_done, gate_ready, fv_done, gated, final_ready = (sem("r_done"), sem("gate_ready"), sem("fv_done"),
                                                           sem("gated"), sem("final_ready"))
        stored = sem("stored")

        E_BANKS, S_BANKS, T_BANKS, O_BANK = (0, 1, 2), (0, 1), (4, 5), 3

        dense, turn, late = {}, 0, False
        for piece in order("tensor"):
            if piece[0] in ("k", "q", "v", "vt", "o", "t2", "fk", "r", "fv"):
                dense[piece] = bank[(2, 6, 7, 0, 1, 3, 4, 5)[turn % (8 if late else 3)]]
                turn += 1
            if piece == ("attend", PAIRS - 1):
                turn, late = 3 if turn % 3 == 0 else 3 + turn % 3, True

        def mix_tokens(u):
            return MIX_TILES[u] * P, MIX_TILES[u + 1] * P

        def pair_place(p):
            half, chunk, m = p // 4, (p // 2) % 2, p % 2
            return chunk, (half * 2 + m) * 32, chunk * 4 + half * 2 + m

        def value_heads(n, odd):
            b = dense["vt", n][odd * HALF:(odd + 1) * HALF, :]
            return b.rearrange("p (b h o d) -> p b h o d", b=2, o=2, d=HEAD_DIM)[:, :, :, odd]

        def value_slots(n, odd):
            rows = vb[odd * HALF:(odd + 1) * HALF, (n // GP) % 2, 2 * (n % GP):2 * (n % GP) + 2]
            return rows[:, :, :, odd * HEAD_DIM:(odd + 1) * HEAD_DIM]

        def shifted(u):
            (at, end), runs = mix_tokens(u), []
            while at < end:
                q = at % SEQ
                if q == 0 and end - at >= SEQ:
                    n = (end - at) // SEQ
                    runs.append((at + 1, n, SEQ - 1))
                    at += n * SEQ
                else:
                    upto = min(end, at - q + SEQ)
                    at += q == 0
                    runs.append((at, 1, upto - at))
                    at = upto
            return runs

        block = ctx.enter_context(nc.Block())

        @block.sync
        def _(sp):
            def load_pixels(t):
                if t >= PIX_RAW:
                    sp.wait_ge(*((pix_lo, t - PIX_RAW) if t > PIX_RAW else (first_lo, W_TOK_PARTS)))
                sp.dma_start(pix_raw[:, t % PIX_RAW], patches[t]).then_inc(dma_pix[t], 16)

            def load_weight(n):
                sp.dma_start(w_raw[:, n], (w_k, w_q, w_v, w_o, w_fk, w_r, w_fv)[n]).then_inc(dma_w[n], 16)

            part = PC // W_TOK_PARTS
            for n in range(W_TOK_PARTS):
                sp.dma_start(tok_w_raw[:, n * part:(n + 1) * part], w_tok[:, n * part:(n + 1) * part]
                             ).then_inc(dma_wtok[n], 16)
                sp.dma_start(pix_raw[:, 0, n * part:(n + 1) * part], patches[0][:, n * part:(n + 1) * part]
                             ).then_inc(dma_first[n], 16)
            for t in range(1, PIX_RAW):
                load_pixels(t)
                if t == 1:
                    sp.dma_start(tok_bias[:], b_tok.to_broadcast([P, DIM])).then_inc(dma_bias, 16)
                    sp.dma_start(const[:], consts).then_inc(dma_const, 16)
                else:
                    load_weight(W_ORDER[t - 2])
            sp.dma_start(cols[:], columns).then_inc(dma_cols, 16)
            for t in range(PIX_RAW, TILES):
                load_pixels(t)
                load_weight(W_ORDER[t - 2])
            sp.dma_start(o_bias[:], b_o.to_broadcast([P, DIM])).then_inc(dma_o_bias, 16)
            for t in range(TILES):
                sp.wait_ge(final_ready, t + 1)
                sp.dma_start(out[t * P:(t + 1) * P, :], h[:, t]).then_inc(stored, 16)
            sp.wait_ge(stored, 16 * TILES)

        @block.scalar
        def _(act):
            def weight_hi(n):
                n = W_ORDER[n]
                act.wait_ge(dma_w[n], 16)
                nc.scalar.activation(w[:, n, HI], w_raw[:, n], ACT.Copy, scale=0.5 if n == WFV else 1.0).then_inc(w_hi, 1)

            def pixels_hi(t):
                act.wait_ge(dma_pix[t], 16)
                if t >= PIX_SPLIT:
                    act.wait_ge(embedded, t - PIX_SPLIT + 1)
                nc.scalar.activation(pix[:, t % PIX_SPLIT, HI], pix_raw[:, t % PIX_RAW], ACT.Copy).then_inc(pix_hi, 1)

            def y1_high(t):
                act.wait_ge(norm_transposed, t + 1)
                nc.scalar.activation(y1[:, HI, :, t * P:(t + 1) * P],
                                     bank[T_BANKS[t % 2]][:, 0:DIM].rearrange("p (c n) -> p c n", c=FC),
                                     ACT.Copy).then_inc(y1_hi, 1)

            def exponentials(i):
                act.wait_ge(diff_ready, 2 * i + 2)
                if i == 0:
                    act.wait_ge(probs_zeroed, 1)
                if i >= 3:
                    act.wait_ge(probs_transposed, 2 * (i - 2))
                nc.scalar.activation(probs[:, i % 3, :, 0:SEQ], diff[:, i % 2], ACT.Exp,
                                     scale=HEAD_DIM ** -0.5).then_inc(exp_ready, 1)

            def probs_out(i):
                for part in range(2):
                    act.wait_ge(probs_transposed, 2 * i + part + 1)
                    if i >= 2:
                        act.wait_ge(attended, i - 1)
                    nc.scalar.activation(pT[:, i % 2, 4 * part:4 * part + 4],
                                         bank[T_BANKS[part]][:, :].rearrange("p (h b q) -> p h b q", h=4, b=2)
                                         [:, :, :, 0:SEQ], ACT.Copy).then_inc(pT_ready, 1)

            def attention_high(i):
                act.wait_ge(attended, i + 1)
                nc.scalar.activation(attn[:, HI, :, i * 2 * SEQ:(i + 1) * 2 * SEQ],
                                     bank[O_BANK][:, 0:FC * 2 * SEQ].rearrange("p (c n) -> p c n", c=FC),
                                     ACT.Copy).then_inc(attn_hi, 1)

            def start():
                part = PC // W_TOK_PARTS
                for n in range(W_TOK_PARTS):
                    act.wait_ge(dma_wtok[n], 16)
                    nc.scalar.activation(tok_w[:, HI, n * part:(n + 1) * part],
                                         tok_w_raw[:, n * part:(n + 1) * part], ACT.Copy).then_inc(wtok_hi, 1)
                    act.wait_ge(dma_first[n], 16)
                    nc.scalar.activation(pix[:, 0, HI, n * part:(n + 1) * part],
                                         pix_raw[:, 0, n * part:(n + 1) * part], ACT.Copy).then_inc(first_hi, 1)

            for kind, *a in order("scalar"):
                if kind == "start":
                    start()
                if kind == "pixels":
                    pixels_hi(*a)
                if kind == "weight":
                    weight_hi(*a)
                if kind == "y1":
                    y1_high(*a)
                if kind == "exp":
                    exponentials(*a)
                if kind == "probs":
                    probs_out(*a)
                if kind == "attention":
                    attention_high(*a)
                if kind in ("k", "q", "v") and a == [0, 0]:
                    act.wait_ge(dma_cols, 16)
                    act.wait_ge(zeroed, 4)
                if kind == "k":
                    g, c = a
                    act.wait_ge(k_done, FC * g + c + 1)
                    if g:
                        act.wait_ge(k_ready, FC * (g - 1) + c + 1)
                        act.wait_ge(k_last_ready, FC * (g - 1) + c + 1)
                    nc.scalar.activation(k_raw[:, c], dense["k", g, c][:, 0:GROUP], ACT.Identity,
                                         bias=bk[:, c:c + 1]).then_inc(k_raw_ready, 1)
                if kind == "q":
                    g, c = a
                    act.wait_ge(q_done, FC * g + c + 1)
                    if g >= 2:
                        act.wait_ge(scored, 2 * GP * (g - 1))
                    for half in range(2):
                        rows = slice(half * HALF, (half + 1) * HALF)
                        last = nc.scalar.activation(qT[rows, g % 2, c, half], dense["q", g, c][rows, 0:GROUP],
                                                    ACT.Identity, bias=bq[rows, c:c + 1])
                    last.then_inc(q_ready, 1)
                if kind == "v":
                    g, c = a
                    act.wait_ge(v_done, FC * g + c + 1)
                    if g:
                        act.wait_ge(vt_done, GP * g)
                    nc.scalar.activation(vT[:, c, :, :, 0:SEQ],
                                         dense["v", g, c][:, 0:GROUP].rearrange("p (b k) -> p b k", b=GB)
                                         .unsqueeze(2).to_broadcast([P, GB, 2, SEQ]),
                                         ACT.Identity, bias=bv[:, c:c + 1]).then_inc(vT_ready, 1)
                if kind == "vt":
                    n, = a
                    act.wait_ge(vt_done, n + 1)
                    if n >= 2 * GP:
                        act.wait_ge(attended, n - 2 * GP + 1)
                    nc.scalar.activation(value_slots(n, 0), value_heads(n, 0), ACT.Copy).then_inc(v_even_ready, 1)
                    nc.scalar.activation(value_slots(n, 1), value_heads(n, 1), ACT.Copy).then_inc(v_odd_ready, 1)
                if kind == "t2":
                    t, = a
                    act.wait_ge(norm_transposed, TILES + t + 1)
                    nc.scalar.activation(y2[:, :, t * P:(t + 1) * P],
                                         dense["t2", t][:, 0:DIM].rearrange("p (c n) -> p c n", c=FC),
                                         ACT.Copy).then_inc(y2_ready, 1)
                if kind == "scale":
                    u, which = a
                    lo, hi = mix_tokens(u)
                    act.wait_ge(y2_ready, MIX_TILES[u + 1])
                    for c in range(FC):
                        if u:
                            act.wait_ge(mixed_lo[which], FC * (u - 1) + c + 1)
                        nc.scalar.activation(mix_sum[:, which, c, 0:hi - lo], y2[:, c, lo:hi], ACT.Copy,
                                             scale=mu[:, which, c:c + 1]).then_inc(scaled[which], 1)
                if kind == "high":
                    u, which = a
                    lo, hi = mix_tokens(u)
                    if u >= 2:
                        act.wait_ge(*((fk_done, FC * (u - 1)), (r_done, MIX_TILES[u - 1]))[which])
                    for c in range(FC):
                        act.wait_ge(mix_ready[which], FC * u + c + 1)
                        nc.scalar.activation(mixed[:, u % 2, which, HI, c, 0:hi - lo], mix_sum[:, which, c, 0:hi - lo],
                                             ACT.Copy).then_inc(mixed_hi[which], 1)
                if kind == "fk":
                    u, c = a
                    n = FC * u + c
                    lo, hi = mix_tokens(u)
                    act.wait_ge(fk_done, n + 1)
                    if u:
                        act.wait_ge(square_ready, n - FC + 1)
                        act.wait_ge(fv_done, MIX_TILES[u])
                    nc.scalar.activation(relu[:, c, 0:hi - lo], dense["fk", u, c][:, 0:hi - lo], ACT.Relu
                                         ).then_inc(relu_ready, 1)
                    act.wait_ge(relu_ready, n + 1)
                    nc.scalar.activation(keys_sq[:, HI, c, 0:hi - lo], relu[:, c, 0:hi - lo], ACT.Square).then_inc(keys_hi, 1)
                if kind == "r":
                    t, = a
                    act.wait_ge(r_done, t + 1)
                    if t >= MIX_MAX:
                        act.wait_ge(final_ready, t - MIX_MAX + 1)
                    nc.scalar.activation(gate[:, t % MIX_MAX], dense["r", t][:, 0:DIM], ACT.Tanh,
                                         scale=0.5).then_inc(gate_ready, 1)

        @block.gpsimd
        def _(pool):
            nc.gpsimd.memset(power[:], -0.5).then_inc(zeroed, 1)
            nc.gpsimd.memset(vT[:, :, :, :, SEQ:].rearrange("p c b o k -> p (c b o) k"), 0.0).then_inc(zeroed, 1)

            nc.gpsimd.memset(qT[:], 0.0).then_inc(zeroed, 1)
            nc.gpsimd.memset(vb[:], 0.0).then_inc(zeroed, 1)

            def weight_lo(n):
                pool.wait_ge(w_hi, n + 1)
                n = W_ORDER[n]
                nc.gpsimd.tensor_tensor(w[:, n, LO], w_raw[:, n], w[:, n, HI].bitcast(f32),
                                        ALU.subtract).then_inc(w_lo, 1)

            def rstds(which, t):
                n = which * TILES + t
                pool.wait_ge(stats_ready, n + 1)
                nc.gpsimd.tensor_scalar(var_eps[:, which, t:t + 1], moments[:, which, t, 1:2], LN_EPS, None,
                                        ALU.add).then_inc(eps_added, 1)
                pool.wait_ge(eps_added, n + 1)
                nc.gpsimd.tensor_tensor(rstd[:, which, t:t + 1], var_eps[:, which, t:t + 1], power[:],
                                        ALU.pow).then_inc(rstd_ready, 1)

            pool.wait_ge(zeroed, 2)
            for kind, *a in order("gpsimd"):
                if kind == "weight" and a[0] < W_ORDER.index(WFV):
                    weight_lo(*a)
                if kind == "rstd1":
                    rstds(0, *a)
                if kind == "rstd2":
                    rstds(1, *a)
                if kind == "zero":
                    pool.wait_ge(w_lo, 7)
                    pool.wait_ge(h_ready, TILES)
                    nc.gpsimd.memset(probs[:, :, :, SEQ:].rearrange("p r s k -> p (r s) k"), 0.0
                                     ).then_inc(probs_zeroed, 1)
                if kind == "divide":
                    i, = a
                    pool.wait_ge(inv_ready, i + 1)
                    nc.gpsimd.tensor_tensor(probs[:, i % 3, :, 0:SEQ], probs[:, i % 3, :, 0:SEQ],
                                            row_inv[:, i % 2].unsqueeze(2).to_broadcast([P, HEADS, SEQ]),
                                            ALU.mult).then_inc(probs_ready, 1)
                if kind == "gate_low":
                    (u,), which = a, GATE
                    lo, hi = mix_tokens(u)
                    for c in range(FC):
                        pool.wait_ge(mixed_hi[which], FC * u + c + 1)
                        nc.gpsimd.tensor_tensor(mixed[:, u % 2, which, LO, c, 0:hi - lo], mix_sum[:, which, c, 0:hi - lo],
                                                mixed[:, u % 2, which, HI, c, 0:hi - lo].bitcast(f32),
                                                ALU.subtract).then_inc(mixed_lo[which], 1)
                if kind == "early_out":
                    t, = a
                    pool.wait_ge(gated, t + 1)
                    nc.gpsimd.tensor_tensor(h[:, t], gate[:, t % MIX_MAX], h[:, t], ALU.add).then_inc(final_ready, 1)
                if kind == "residual":
                    t, = a
                    if t == 0:
                        pool.wait_ge(dma_o_bias, 16)
                    pool.wait_ge(normed_ready, t + 1)
                    nc.gpsimd.tensor_tensor(h[:, t], h[:, t], o_bias[:], ALU.add).then_inc(resid_ready, 1)
                if kind == "k":
                    g, c = a
                    if g == 0 and c == 0:
                        pool.wait_ge(dma_const, 16)
                    pool.wait_ge(k_raw_ready, FC * g + c + 1)
                    if g >= 2:
                        pool.wait_ge(scored, 2 * GP * (g - 1))
                    for m in range(QUAD - 2, QUAD):
                        last = nc.gpsimd.tensor_scalar(km[:, g % 2, c, m], k_raw[:, c], head_mask[:, m:m + 1], 0.0,
                                                       ALU.mult, ALU.add)
                    last.then_inc(k_last_ready, 1)

        @block.vector
        def _(dve):
            def pixels_lo(t):
                dve.wait_ge(pix_hi, t)
                nc.vector.tensor_tensor(pix[:, t % PIX_SPLIT, LO], pix_raw[:, t % PIX_RAW], pix[:, t % PIX_SPLIT, HI].bitcast(f32),
                                        ALU.subtract).then_inc(pix_lo, 1)

            def tile_stats(which, t):
                n = which * TILES + t
                dve.wait_ge(h_ready, n + 1)
                nc.vector.bn_stats(stats[:, which, t], h[:, t]).then_inc(bn_done, 1)

            def tile_moments(which, t):
                n = which * TILES + t
                dve.wait_ge(bn_done, n + 1)
                nc.vector.bn_aggr(moments[:, which, t], stats[:, which, t]).then_inc(stats_ready, 1)

            def normalise(which, t):
                n = which * TILES + t
                dve.wait_ge(rstd_ready, n + 1)
                if n >= 2:
                    dve.wait_ge(norm_transposed, n - 1)
                nc.vector.tensor_scalar(normed[:, n % 2], h[:, t], moments[:, which, t, 0:1],
                                        rstd[:, which, t:t + 1], ALU.subtract, ALU.mult).then_inc(normed_ready, 1)

            def y1_low(t):
                dve.wait_ge(y1_hi, t + 1)
                tokens = slice(t * P, (t + 1) * P)
                nc.vector.tensor_tensor(y1[:, LO, :, tokens],
                                        bank[T_BANKS[t % 2]][:, 0:DIM].rearrange("p (c n) -> p c n", c=FC),
                                        y1[:, HI, :, tokens].bitcast(f32), ALU.subtract).then_inc(y1_lo, 1)

            def softmax_scores(i, half):
                n = 2 * i + half
                scores = bank[S_BANKS[half]][:, 0:8 * SEQ].rearrange("p (s k) -> p s k", k=SEQ)
                heads = slice(8 * half, 8 * half + 8)
                dve.wait_ge(scored, n + 1)
                nc.vector.tensor_reduce(row_max[:, i % 2, heads], scores, AX.X, ALU.max).then_inc(max_ready, 1)
                dve.wait_ge(max_ready, n + 1)
                if i >= 2:
                    dve.wait_ge(exp_ready, i - 1)
                nc.vector.tensor_tensor(diff[:, i % 2, heads], scores,
                                        row_max[:, i % 2, heads].unsqueeze(2).to_broadcast([P, 8, SEQ]),
                                        ALU.subtract).then_inc(diff_ready, 1)

            def softmax_sums(i):
                dve.wait_ge(exp_ready, i + 1)
                nc.vector.tensor_reduce(row_sum[:, i % 2], probs[:, i % 3, :, 0:SEQ], AX.X,
                                        ALU.add).then_inc(sum_ready, 1)
                dve.wait_ge(sum_ready, i + 1)
                if i >= 2:
                    dve.wait_ge(probs_ready, i - 1)
                nc.vector.reciprocal(row_inv[:, i % 2], row_sum[:, i % 2]).then_inc(inv_ready, 1)

            def attention_low(i):
                dve.wait_ge(attn_hi, i + 1)
                tokens = slice(i * 2 * SEQ, (i + 1) * 2 * SEQ)
                nc.vector.tensor_tensor(attn[:, LO, :, tokens],
                                        bank[O_BANK][:, 0:FC * 2 * SEQ].rearrange("p (c n) -> p c n", c=FC),
                                        attn[:, HI, :, tokens].bitcast(f32), ALU.subtract).then_inc(attn_lo, 1)

            def start():
                part = PC // W_TOK_PARTS
                for n in range(W_TOK_PARTS):
                    dve.wait_ge(wtok_hi, n + 1)
                    chunks = slice(n * part, (n + 1) * part)
                    nc.vector.tensor_tensor(tok_w[:, LO, chunks], tok_w_raw[:, chunks],
                                            tok_w[:, HI, chunks].bitcast(f32), ALU.subtract).then_inc(wtok_lo, 1)
                    dve.wait_ge(first_hi, n + 1)
                    nc.vector.tensor_tensor(pix[:, 0, LO, chunks], pix_raw[:, 0, chunks],
                                            pix[:, 0, HI, chunks].bitcast(f32), ALU.subtract).then_inc(first_lo, 1)

            nc.vector.memset(causal_bf[:], 0.0).then_inc(warm_ready, 1)
            for kind, *a in order("vector"):
                if kind == "start":
                    start()
                if kind == "pixels":
                    pixels_lo(*a)
                if kind == "h1":
                    t, = a
                    if t == 0:
                        dve.wait_ge(dma_bias, 16)
                    dve.wait_ge(embedded, t + 1)
                    nc.vector.tensor_tensor(h[:, t], bank[E_BANKS[t % 3]][:, 0:DIM], tok_bias[:],
                                            ALU.add).then_inc(h_ready, 1)
                if kind == "stats1":
                    tile_stats(0, *a)
                if kind == "moments1":
                    tile_moments(0, *a)
                if kind == "norm1":
                    normalise(0, *a)
                if kind == "y1":
                    y1_low(*a)
                if kind == "weight_v":
                    dve.wait_ge(w_hi, 7)
                    dve.wait_ge(w_lo, 6)
                    nc.vector.scalar_tensor_tensor(w[:, WFV, LO], w_raw[:, WFV], 0.5, w[:, WFV, HI].bitcast(f32),
                                                   ALU.mult, ALU.subtract).then_inc(w_lo, 1)
                if kind == "constants":
                    dve.wait_ge(dma_const, 16)
                    dve.wait_ge(dma_cols, 16)
                    dve.wait_ge(warmed, 1)
                    nc.vector.tensor_copy(ident_bf[:], ident).then_inc(bf_ready, 1)
                    nc.vector.tensor_copy(causal_bf[:], causal.unsqueeze(1).to_broadcast([P, GB, SEQ])
                                          ).then_inc(bf_ready, 1)
                    nc.vector.tensor_scalar(one_less_mu[:], mu, -1.0, 1.0, ALU.mult, ALU.add).then_inc(less_ready, 1)
                if kind == "scores":
                    softmax_scores(*a)
                if kind == "sums":
                    softmax_sums(*a)
                if kind == "attention":
                    attention_low(*a)
                if kind == "k":
                    g, c = a
                    dve.wait_ge(k_raw_ready, FC * g + c + 1)
                    if g >= 2:
                        dve.wait_ge(scored, 2 * GP * (g - 1))
                    for m in range(QUAD - 2):
                        last = nc.vector.tensor_scalar(km[:, g % 2, c, m], k_raw[:, c], head_mask[:, m:m + 1], None,
                                                       ALU.mult)
                    last.then_inc(k_ready, 1)
                if kind == "o":
                    t, = a
                    dve.wait_ge(projected, t + 1)
                    dve.wait_ge(resid_ready, t + 1)
                    nc.vector.tensor_tensor(h[:, t], dense["o", t][:, 0:DIM], h[:, t],
                                            ALU.add).then_inc(h_ready, 1)
                    tile_stats(1, t)
                    tile_moments(1, t)
                if kind == "norm2":
                    normalise(1, *a)
                if kind == "sum":
                    u, which = a
                    dve.wait_ge(less_ready, 1)
                    for c in range(FC):
                        dve.wait_ge(scaled[which], FC * u + c + 1)
                        for first, batches, length in shifted(u):
                            at = first - mix_tokens(u)[0]
                            if batches > 1:
                                here = mix_sum[:, which, c, at - 1:at - 1 + batches * SEQ]
                                before = y2[:, c, first - 1:first - 1 + batches * SEQ]
                                here = here.rearrange("p (b q) -> p b q", q=SEQ)[:, :, 1:]
                                before = before.rearrange("p (b q) -> p b q", q=SEQ)[:, :, 0:SEQ - 1]
                            else:
                                here = mix_sum[:, which, c, at:at + length]
                                before = y2[:, c, first - 1:first - 1 + length]
                            last = nc.vector.scalar_tensor_tensor(here, before, one_less_mu[:, which, c:c + 1], here,
                                                                  ALU.mult, ALU.add)
                        last.then_inc(mix_ready[which], 1)
                if kind == "keys_low":
                    (u,), which = a, KEYS
                    lo, hi = mix_tokens(u)
                    for c in range(FC):
                        dve.wait_ge(mixed_hi[which], FC * u + c + 1)
                        nc.vector.tensor_tensor(mixed[:, u % 2, which, LO, c, 0:hi - lo], mix_sum[:, which, c, 0:hi - lo],
                                                mixed[:, u % 2, which, HI, c, 0:hi - lo].bitcast(f32),
                                                ALU.subtract).then_inc(mixed_lo[which], 1)
                if kind == "fk":
                    u, c = a
                    n = FC * u + c
                    lo, hi = mix_tokens(u)
                    now = slice(0, hi - lo)
                    dve.wait_ge(relu_ready, n + 1)
                    nc.vector.tensor_tensor(square[:, c, now], relu[:, c, now], relu[:, c, now],
                                            ALU.mult).then_inc(square_ready, 1)
                    dve.wait_ge(square_ready, n + 1)
                    dve.wait_ge(keys_hi, n + 1)
                    nc.vector.tensor_tensor(keys_sq[:, LO, c, now], square[:, c, now], keys_sq[:, HI, c, now].bitcast(f32),
                                            ALU.subtract).then_inc(keys_lo, 1)
                if kind == "fv":
                    t, = a
                    dve.wait_ge(fv_done, t + 1)
                    dve.wait_ge(gate_ready, t + 1)
                    nc.vector.scalar_tensor_tensor(gate[:, t % MIX_MAX], gate[:, t % MIX_MAX], 1.0,
                                                   dense["fv", t][:, 0:DIM],
                                                   ALU.add, ALU.mult).then_inc(gated, 1)
                    if t >= EARLY_OUT:
                        dve.wait_ge(gated, t + 1)
                        if t == EARLY_OUT:
                            dve.wait_ge(final_ready, EARLY_OUT)
                        nc.vector.tensor_tensor(h[:, t], gate[:, t % MIX_MAX], h[:, t], ALU.add).then_inc(final_ready, 1)

        @block.tensor
        def _(pe):
            emptied = {b.name: () for b in bank}

            def claim(b, *reads):
                for semaphore, count in emptied[b.name]:
                    pe.wait_ge(semaphore, count)
                emptied[b.name] = reads

            def product(result, chunks, stationary, moving):
                for f in range(chunks):
                    for n, (a, b) in enumerate(PASSES):
                        last = nc.tensor.matmul(result, stationary(a, f), moving(b, f),
                                                start=(f == 0 and n == 0), stop=(f == chunks - 1 and n == 2))
                return last

            def embed(t):
                claim(bank[E_BANKS[t % 3]], (h_ready, t + 1))
                if t:
                    pe.wait_ge(pix_lo, t)
                part = PC // W_TOK_PARTS
                for c in range(PC):
                    if t == 0 and c % part == 0:
                        pe.wait_ge(wtok_lo, c // part + 1)
                        pe.wait_ge(first_lo, c // part + 1)
                    for n, (a, b) in enumerate(PASSES):
                        last = nc.tensor.matmul(bank[E_BANKS[t % 3]][:, 0:DIM], pix[:, t % PIX_SPLIT, a, c], tok_w[:, b, c],
                                                start=(c == 0 and n == 0), stop=(c == PC - 1 and n == 2))
                last.then_inc(embedded, 1)

            def transpose_norm(which, t, b):
                n = which * TILES + t
                pe.wait_ge(normed_ready, n + 1)
                for c in range(FC):
                    last = nc.tensor.transpose(b[:, c * P:(c + 1) * P], normed[:, n % 2, c * P:(c + 1) * P], ident)
                last.then_inc(norm_transposed, 1)

            def score(i, half):
                n = 2 * i + half
                b = bank[S_BANKS[half]]
                g, first = i // GP, (i % GP) * 2
                pe.wait_ge(q_ready, FC * (g + 1))
                pe.wait_ge(k_ready, FC * (g + 1))
                pe.wait_ge(k_last_ready, FC * (g + 1))
                if n == 0:
                    pe.wait_ge(bf_ready, 2)
                claim(b, (diff_ready, n + 1))
                nc.tensor.matmul(b[:, 0:8 * SEQ], ident_bf[:], causal_bf[:].rearrange("p s k -> p (s k)"),
                                 start=True, stop=False, skip_group_check=True)
                for c in range(FC):
                    for e in range(2):
                        tok = slice((first + e) * SEQ, (first + e + 1) * SEQ)
                        last = nc.tensor.matmul(b[e * HALF:e * HALF + SEQ, c * 4 * SEQ:(c + 1) * 4 * SEQ],
                                                qT[:, g % 2, c, half, tok], km[:, g % 2, c, :, tok],
                                                start=False, stop=True, skip_group_check=True)
                last.then_inc(scored, 1)

            def transpose_probs(i):
                pe.wait_ge(probs_ready, i + 1)
                for part in range(2):
                    b = bank[T_BANKS[part]]
                    claim(b, (pT_ready, 2 * i + part + 1))
                    for p in range(4):
                        pair = probs[0:ROWS, i % 3, 8 * part + 2 * p:8 * part + 2 * p + 2]
                        last = nc.tensor.transpose(b[:, p * P:p * P + ROWS], pair.rearrange("p h k -> p (h k)"),
                                                   ident[0:ROWS, 0:ROWS])
                    last.then_inc(probs_transposed, 1)

            def attend(i):
                pe.wait_ge(pT_ready, 2 * i + 2)
                pe.wait_ge(v_even_ready, i + 1)
                pe.wait_ge(v_odd_ready, i + 1)
                claim(bank[O_BANK], (attn_lo, i + 1))
                for e in range(2):
                    for p in range(HEAD_PAIRS):
                        c, row, true_pair = pair_place(p)
                        last = nc.tensor.matmul(
                            bank[O_BANK][row:row + 32, (c * 2 + e) * SEQ:(c * 2 + e + 1) * SEQ],
                            vb[:, (i // GP) % 2, 2 * (i % GP) + e, true_pair], pT[:, i % 2, p, e], start=True, stop=True,
                            tile_position=(0, row), skip_group_check=True)
                last.then_inc(attended, 1)

            pe.wait_ge(warm_ready, 1)
            zeros = causal_bf[:].rearrange("p s k -> p (s k)")
            for n in range(WARM_UP):
                last = nc.tensor.matmul(bank[7][:, 0:GROUP], zeros[:, 0:P], zeros, start=True, stop=True)
            last.then_inc(warmed, 1)

            for kind, *a in order("tensor"):
                if kind == "embed":
                    embed(*a)
                if kind == "t1":
                    t, = a
                    if t == 0:
                        pe.wait_ge(dma_const, 16)
                    claim(bank[T_BANKS[t % 2]], (y1_lo, t + 1))
                    transpose_norm(0, t, bank[T_BANKS[t % 2]])
                if kind == "score":
                    score(*a)
                if kind == "attend":
                    attend(*a)
                if kind == "transpose":
                    transpose_probs(*a)
                b = dense.get((kind, *a))
                if kind in ("k", "q", "v"):
                    g, c = a
                    n, done, read = {"k": (WK, k_done, k_raw_ready), "q": (WQ, q_done, q_ready),
                                     "v": (WV, v_done, vT_ready)}[kind]
                    claim(b, (read, FC * g + c + 1))
                    pe.wait_ge(w_lo, W_ORDER.index(n) + 1)
                    pe.wait_ge(y1_lo, -(-(g + 1) * GROUP // P))
                    product(b[:, 0:GROUP], FC, lambda x, f: w[:, n, x, f, c * P:(c + 1) * P],
                            lambda x, f: y1[:, x, f, g * GROUP:(g + 1) * GROUP]).then_inc(done, 1)
                if kind == "vt":
                    n, = a
                    claim(b, (v_even_ready, n + 1), (v_odd_ready, n + 1))
                    pe.wait_ge(vT_ready, FC * (n // GP + 1))
                    for e in range(2):
                        for c in range(FC):
                            last = nc.tensor.transpose(b[:, (e * FC + c) * P:(e * FC + c + 1) * P],
                                                       vT[:, c, (2 * n + e) % GB].rearrange("p o k -> p (o k)"), ident)
                    last.then_inc(vt_done, 1)
                if kind == "o":
                    t, = a
                    claim(b, (h_ready, TILES + t + 1))
                    pe.wait_ge(w_lo, WO + 1)
                    pe.wait_ge(attn_lo, -(-(t + 1) * P // (2 * SEQ)))
                    product(b[:, 0:DIM], FC, lambda x, f: attn[:, x, f, t * P:(t + 1) * P],
                            lambda x, f: w[:, WO, x, f]).then_inc(projected, 1)
                if kind == "t2":
                    t, = a
                    claim(b, (y2_ready, t + 1))
                    transpose_norm(1, t, b)
                if kind == "fk":
                    u, c = a
                    claim(b, (relu_ready, FC * u + c + 1))
                    pe.wait_ge(mixed_lo[0], FC * (u + 1))
                    n = mix_tokens(u)[1] - mix_tokens(u)[0]
                    product(b[:, 0:n], FC, lambda x, f: w[:, WFK, x, f, c * P:(c + 1) * P],
                            lambda x, f: mixed[:, u % 2, 0, x, f, 0:n]).then_inc(fk_done, 1)
                if kind == "r":
                    t, = a
                    u = max(n for n in range(MIXES) if MIX_TILES[n] <= t)
                    at = (t - MIX_TILES[u]) * P
                    claim(b, (gate_ready, t + 1))
                    pe.wait_ge(mixed_lo[1], FC * (u + 1))
                    product(b[:, 0:DIM], FC, lambda x, f: mixed[:, u % 2, 1, x, f, at:at + P],
                            lambda x, f: w[:, WR, x, f]).then_inc(r_done, 1)
                if kind == "fv":
                    t, = a
                    u = max(n for n in range(MIXES) if MIX_TILES[n] <= t)
                    at = (t - MIX_TILES[u]) * P
                    claim(b, (gated, t + 1))
                    pe.wait_ge(keys_lo, FC * (u + 1))
                    product(b[:, 0:DIM], FC, lambda x, f: keys_sq[:, x, f, at:at + P],
                            lambda x, f: w[:, WFV, x, f]).then_inc(fv_done, 1)


def kernel(x, L0_tok_W, L0_tok_b, L0_attn_Wq, L0_attn_bq, L0_attn_Wk, L0_attn_bk, L0_attn_Wv, L0_attn_bv,
           L0_attn_Wo, L0_attn_bo, L0_ffn_W_r, L0_ffn_W_k, L0_ffn_W_v, L0_ffn_mu_r, L0_ffn_mu_k):
    import numpy as np
    import concourse.bacc as bacc
    from concourse.bass_utils import run_bass_kernel_spmd

    def weight(w, chunks):
        return np.ascontiguousarray(np.asarray(w).T.reshape(chunks, P, DIM).transpose(1, 0, 2))

    def column(v):
        return np.ascontiguousarray(np.asarray(v).reshape(FC, P).T)

    pixels = np.asarray(x).reshape(BATCH, CHANNELS, GRID, PATCH, GRID, PATCH).transpose(1, 3, 5, 0, 2, 4)
    pixels = pixels.reshape(PC, P, TILES, P).transpose(2, 1, 0, 3)

    row = np.arange(P)[:, None]
    blocked = (np.arange(SEQ)[None, :] > row % HALF) & (row % HALF < SEQ)
    consts = np.concatenate([np.eye(P), np.where(blocked, MASKED, 0.0),
                             row // HEAD_DIM % QUAD == np.arange(QUAD)[None, :]], axis=1).astype(np.float32)

    arrays = dict(zip(INPUTS, [
        np.ascontiguousarray(pixels), weight(L0_tok_W, PC),
        *(weight(w, FC) for w in (L0_attn_Wk, L0_attn_Wq, L0_attn_Wv, L0_attn_Wo, L0_ffn_W_k, L0_ffn_W_r, L0_ffn_W_v)),
        np.asarray(L0_tok_b).reshape(1, DIM), np.asarray(L0_attn_bo).reshape(1, DIM),
        np.ascontiguousarray(np.stack([column(v) for v in (L0_attn_bq, L0_attn_bk, L0_attn_bv, L0_ffn_mu_k,
                                                           L0_ffn_mu_r)], axis=1)), consts]))

    nc = bacc.Bacc("TRN2", target_bir_lowering=False, num_devices=1)
    args = [nc.dram_tensor(n, a.shape, mybir.dt.from_np(a.dtype), kind="ExternalInput").ap()
            for n, a in arrays.items()]
    out = nc.dram_tensor("out", (TOKENS, DIM), mybir.dt.float32, kind="ExternalOutput").ap()
    vit_tower(nc, *args, out)
    result = run_bass_kernel_spmd(nc, [arrays], core_ids=[0])
    return result.results[0]["out"].reshape(BATCH, SEQ, DIM)
```
